# Optimizing a Trainium2 kernel written in Bass

```python
import numpy as np
import jax
import jax.numpy as jnp

def _softmax(x, axis=-1):
    return jax.nn.softmax(x, axis=axis)

def _gelu(x):
    return jax.nn.gelu(x, approximate=True)

def _silu(x):
    return jax.nn.silu(x)

def _sigmoid(x):
    return jax.nn.sigmoid(x)

def _layernorm(x, axis=-1, eps=1e-05):
    m = jnp.mean(x, axis=axis, keepdims=True)
    v = jnp.var(x, axis=axis, keepdims=True)
    return (x - m) / jnp.sqrt(v + eps)

def _scatter_add(tgt, idx, src, axis=0):
    return tgt.at[idx].add(src)

def _segment_sum(src, seg, n):
    return jax.ops.segment_sum(src, seg, n)
kernel_name = 'mk_adj_seq_d2_adj_r2_86c053'

def setup_inputs(seed: int=0):
    np.random.seed(seed)
    _w = jnp.asarray

    def _rec_inputs():
        import jax
        import jax.numpy as jnp
        _gk = jax.random.key(seed)
        x = -0.000929 + 1 * jax.random.normal(jax.random.fold_in(_gk, 1), (4096, 128), jnp.float32)
        _w = (1.0 + jnp.arange(4096, dtype=jnp.float32)) ** (-0.5)
        _w = _w / _w.mean()
        _pij = jnp.clip(0.00390625 * _w[:, None] * _w[None, :], 0.0, 1.0)
        _a = jax.random.uniform(jax.random.fold_in(_gk, 2), (4096, 4096)) < _pij
        _a = jnp.logical_or(_a, jnp.eye(4096, dtype=bool))
        adj = _a.astype(jnp.int32)
        return (x, adj)
    x, adj = _rec_inputs()

    def _L0_gnn_setup():
        import jax, jax.numpy as jnp
        import numpy as np
        DIM = 128
        HEADS = 8
        DIM_FF = 512
        N = 2048
        HEAD_DIM = DIM // HEADS
        SCALE = HEAD_DIM ** (-0.5)

        def layer_norm(x, gamma, beta, eps=1e-05):
            mu = jnp.mean(x, axis=-1, keepdims=True)
            var = jnp.var(x, axis=-1, keepdims=True)
            return (x - mu) * jax.lax.rsqrt(var + eps) * gamma + beta
        key = jax.random.key(seed)
        ks = jax.random.split(key, 8)
        x = jax.random.normal(ks[0], (N, DIM), dtype=jnp.float32)
        adj = jax.random.randint(ks[1], (N, N), 0, 2, dtype=jnp.int32)
        adj = adj.at[jnp.arange(N), jnp.arange(N)].set(1)
        s = 1.0 / np.sqrt(DIM)
        w_qkv = jax.random.normal(ks[2], (DIM, 3 * DIM), dtype=jnp.float32) * s
        w_proj = jax.random.normal(ks[3], (DIM, DIM), dtype=jnp.float32) * s
        b_proj = jnp.zeros((DIM,), jnp.float32)
        w1 = jax.random.normal(ks[4], (DIM, DIM_FF), dtype=jnp.float32) * s
        b1 = jnp.zeros((DIM_FF,), jnp.float32)
        w2 = jax.random.normal(ks[5], (DIM_FF, DIM), dtype=jnp.float32) / np.sqrt(DIM_FF)
        b2 = jnp.zeros((DIM,), jnp.float32)
        g1 = jnp.ones((DIM,), jnp.float32)
        be1 = jnp.zeros((DIM,), jnp.float32)
        g2 = jnp.ones((DIM,), jnp.float32)
        be2 = jnp.zeros((DIM,), jnp.float32)
        return {'x': x, 'adj': adj, 'w_qkv': w_qkv, 'w_proj': w_proj, 'b_proj': b_proj, 'w1': w1, 'b1': b1, 'w2': w2, 'b2': b2, 'g1': g1, 'be1': be1, 'g2': g2, 'be2': be2}
    _L0_gnn_all = _L0_gnn_setup()
    _L0_gnn_in = {k: v for k, v in _L0_gnn_all.items() if k in ('w_qkv', 'w_proj', 'b_proj', 'w1', 'b1', 'w2', 'b2', 'g1', 'be1', 'g2', 'be2')}
    del _L0_gnn_all

    def _L1_gnn_setup():
        import jax, jax.numpy as jnp
        import numpy as np
        DIM = 128
        HEADS = 8
        DIM_FF = 512
        N = 2048
        HEAD_DIM = DIM // HEADS
        SCALE = HEAD_DIM ** (-0.5)

        def layer_norm(x, gamma, beta, eps=1e-05):
            mu = jnp.mean(x, axis=-1, keepdims=True)
            var = jnp.var(x, axis=-1, keepdims=True)
            return (x - mu) * jax.lax.rsqrt(var + eps) * gamma + beta
        key = jax.random.key(seed)
        ks = jax.random.split(key, 8)
        x = jax.random.normal(ks[0], (N, DIM), dtype=jnp.float32)
        adj = jax.random.randint(ks[1], (N, N), 0, 2, dtype=jnp.int32)
        adj = adj.at[jnp.arange(N), jnp.arange(N)].set(1)
        s = 1.0 / np.sqrt(DIM)
        w_qkv = jax.random.normal(ks[2], (DIM, 3 * DIM), dtype=jnp.float32) * s
        w_proj = jax.random.normal(ks[3], (DIM, DIM), dtype=jnp.float32) * s
        b_proj = jnp.zeros((DIM,), jnp.float32)
        w1 = jax.random.normal(ks[4], (DIM, DIM_FF), dtype=jnp.float32) * s
        b1 = jnp.zeros((DIM_FF,), jnp.float32)
        w2 = jax.random.normal(ks[5], (DIM_FF, DIM), dtype=jnp.float32) / np.sqrt(DIM_FF)
        b2 = jnp.zeros((DIM,), jnp.float32)
        g1 = jnp.ones((DIM,), jnp.float32)
        be1 = jnp.zeros((DIM,), jnp.float32)
        g2 = jnp.ones((DIM,), jnp.float32)
        be2 = jnp.zeros((DIM,), jnp.float32)
        return {'x': x, 'adj': adj, 'w_qkv': w_qkv, 'w_proj': w_proj, 'b_proj': b_proj, 'w1': w1, 'b1': b1, 'w2': w2, 'b2': b2, 'g1': g1, 'be1': be1, 'g2': g2, 'be2': be2}
    _L1_gnn_all = _L1_gnn_setup()
    _L1_gnn_in = {k: v for k, v in _L1_gnn_all.items() if k in ('w_qkv', 'w_proj', 'b_proj', 'w1', 'b1', 'w2', 'b2', 'g1', 'be1', 'g2', 'be2')}
    del _L1_gnn_all
    return {'x': x, 'adj': adj, 'L0_gnn_w_qkv': _L0_gnn_in['w_qkv'], 'L0_gnn_w_proj': _L0_gnn_in['w_proj'], 'L0_gnn_b_proj': _L0_gnn_in['b_proj'], 'L0_gnn_w1': _L0_gnn_in['w1'], 'L0_gnn_b1': _L0_gnn_in['b1'], 'L0_gnn_w2': _L0_gnn_in['w2'], 'L0_gnn_b2': _L0_gnn_in['b2'], 'L0_gnn_g1': _L0_gnn_in['g1'], 'L0_gnn_be1': _L0_gnn_in['be1'], 'L0_gnn_g2': _L0_gnn_in['g2'], 'L0_gnn_be2': _L0_gnn_in['be2'], 'L1_gnn_w_qkv': _L1_gnn_in['w_qkv'], 'L1_gnn_w_proj': _L1_gnn_in['w_proj'], 'L1_gnn_b_proj': _L1_gnn_in['b_proj'], 'L1_gnn_w1': _L1_gnn_in['w1'], 'L1_gnn_b1': _L1_gnn_in['b1'], 'L1_gnn_w2': _L1_gnn_in['w2'], 'L1_gnn_b2': _L1_gnn_in['b2'], 'L1_gnn_g1': _L1_gnn_in['g1'], 'L1_gnn_be1': _L1_gnn_in['be1'], 'L1_gnn_g2': _L1_gnn_in['g2'], 'L1_gnn_be2': _L1_gnn_in['be2']}

def reference(x, adj, L0_gnn_w_qkv, L0_gnn_w_proj, L0_gnn_b_proj, L0_gnn_w1, L0_gnn_b1, L0_gnn_w2, L0_gnn_b2, L0_gnn_g1, L0_gnn_be1, L0_gnn_g2, L0_gnn_be2, L1_gnn_w_qkv, L1_gnn_w_proj, L1_gnn_b_proj, L1_gnn_w1, L1_gnn_b1, L1_gnn_w2, L1_gnn_b2, L1_gnn_g1, L1_gnn_be1, L1_gnn_g2, L1_gnn_be2):
    import jax
    import jax.numpy as jnp

    def _L0_gnn_ref(x, adj, w_qkv, w_proj, b_proj, w1, b1, w2, b2, g1, be1, g2, be2):
        import jax, jax.numpy as jnp
        import numpy as np
        DIM = 128
        HEADS = 8
        DIM_FF = 512
        N = 2048
        HEAD_DIM = DIM // HEADS
        SCALE = HEAD_DIM ** (-0.5)

        def layer_norm(x, gamma, beta, eps=1e-05):
            mu = jnp.mean(x, axis=-1, keepdims=True)
            var = jnp.var(x, axis=-1, keepdims=True)
            return (x - mu) * jax.lax.rsqrt(var + eps) * gamma + beta
        n = x.shape[0]
        qkv = layer_norm(x, g1, be1) @ w_qkv
        qkv = qkv.reshape(n, 3, HEADS, HEAD_DIM)
        q, k, v = (qkv[:, 0], qkv[:, 1], qkv[:, 2])
        scores = jnp.einsum('nhd,mhd->hnm', q, k) * SCALE
        mask = (adj != 0)[None, :, :]
        scores = jnp.where(mask, scores, -jnp.inf)
        attn = jax.nn.softmax(scores, axis=-1)
        out = jnp.einsum('hnm,mhd->nhd', attn, v).reshape(n, DIM)
        x = x + out @ w_proj + b_proj
        h2 = layer_norm(x, g2, be2)
        ff = jax.nn.gelu(h2 @ w1 + b1) @ w2 + b2
        return x + ff

    def _L1_gnn_ref(x, adj, w_qkv, w_proj, b_proj, w1, b1, w2, b2, g1, be1, g2, be2):
        import jax, jax.numpy as jnp
        import numpy as np
        DIM = 128
        HEADS = 8
        DIM_FF = 512
        N = 2048
        HEAD_DIM = DIM // HEADS
        SCALE = HEAD_DIM ** (-0.5)

        def layer_norm(x, gamma, beta, eps=1e-05):
            mu = jnp.mean(x, axis=-1, keepdims=True)
            var = jnp.var(x, axis=-1, keepdims=True)
            return (x - mu) * jax.lax.rsqrt(var + eps) * gamma + beta
        n = x.shape[0]
        qkv = layer_norm(x, g1, be1) @ w_qkv
        qkv = qkv.reshape(n, 3, HEADS, HEAD_DIM)
        q, k, v = (qkv[:, 0], qkv[:, 1], qkv[:, 2])
        scores = jnp.einsum('nhd,mhd->hnm', q, k) * SCALE
        mask = (adj != 0)[None, :, :]
        scores = jnp.where(mask, scores, -jnp.inf)
        attn = jax.nn.softmax(scores, axis=-1)
        out = jnp.einsum('hnm,mhd->nhd', attn, v).reshape(n, DIM)
        x = x + out @ w_proj + b_proj
        h2 = layer_norm(x, g2, be2)
        ff = jax.nn.gelu(h2 @ w1 + b1) @ w2 + b2
        return x + ff
    x = _L0_gnn_ref(x, adj, L0_gnn_w_qkv, L0_gnn_w_proj, L0_gnn_b_proj, L0_gnn_w1, L0_gnn_b1, L0_gnn_w2, L0_gnn_b2, L0_gnn_g1, L0_gnn_be1, L0_gnn_g2, L0_gnn_be2)
    x = _L1_gnn_ref(x, adj, L1_gnn_w_qkv, L1_gnn_w_proj, L1_gnn_b_proj, L1_gnn_w1, L1_gnn_b1, L1_gnn_w2, L1_gnn_b2, L1_gnn_g1, L1_gnn_be1, L1_gnn_g2, L1_gnn_be2)
    return x

_drawn_inputs = setup_inputs


def setup_inputs(seed=0):
    import zlib

    import numpy as np

    out = dict(_drawn_inputs(seed))
    spreads = {'L0_gnn_b_proj': (0.0, 0.1),
     'L0_gnn_b1': (0.0, 0.1),
     'L0_gnn_b2': (0.0, 0.1),
     'L0_gnn_g1': (1.0, 0.2),
     'L0_gnn_be1': (0.0, 0.1),
     'L0_gnn_g2': (1.0, 0.2),
     'L0_gnn_be2': (0.0, 0.1),
     'L1_gnn_b_proj': (0.0, 0.1),
     'L1_gnn_b1': (0.0, 0.1),
     'L1_gnn_b2': (0.0, 0.1),
     'L1_gnn_g1': (1.0, 0.2),
     'L1_gnn_be1': (0.0, 0.1),
     'L1_gnn_g2': (1.0, 0.2),
     'L1_gnn_be2': (0.0, 0.1)}
    factors = {}
    for name, (base, spread) in spreads.items():
        noise = np.random.default_rng([zlib.crc32(name.encode()), seed]).standard_normal(out[name].shape)
        drawn = base * np.exp(spread * noise) if base else spread * noise
        out[name] = jnp.asarray(drawn.astype(out[name].dtype))
    for name, factor in factors.items():
        out[name] = (out[name] * factor).astype(out[name].dtype)
    return out
```

```python
from contextlib import ExitStack

import concourse.bass as bass
from concourse import mybir

ALU = mybir.AluOpType
ACT = mybir.ActivationFunctionType
F32 = mybir.dt.float32
BF16 = mybir.dt.bfloat16
I32 = mybir.dt.int32

P = 128
N = 4096
HEADS, HD = 8, 16
FF = 512
LAYERS = 2
EPS = 1e-5
SCALE = HD ** -0.5

TILE = 512
NB = N // TILE
NS = TILE // P
MT = N // P
MB = N // TILE
STEPS = MT // NS
CHUNK = 1024
NC = N // CHUNK
PARTS = 3
KROWS = 2 * PARTS * HD
MROWS = PARTS * HEADS
MASKED = -1e30
LOWEST = -3e38

Q_PAIRS = (1, 0, 2)
K_PAIRS = (1, 2, 0)

C_QKV, C_PROJ, C_W1, C_W2 = 0, 384, 512, 1024
C_BP, C_B2, C_G1 = 1536, 1664, 1792
C_BE1, C_G2, C_BE2, C_B1 = 1793, 1794, 1795, 1796
WCOLS = 1800

NAMES = ("w_qkv", "w_proj", "b_proj", "w1", "b1", "w2", "b2", "g1", "be1", "g2", "be2")


def gnn_kernel(nc, x, adj, weights, ident, ident_f, head_rows, out):
    ctx = ExitStack()
    with ctx:
        def sb(name, shape, dt):
            return ctx.enter_context(nc.sbuf_tensor(name, shape, dt))

        def sem(name):
            return ctx.enter_context(nc.semaphore(name))

        q_dram = nc.dram_tensor("q_parts_dram", (NB, KROWS, NS, HEADS, P), BF16, kind="Internal").ap()
        o_dram = nc.dram_tensor("attn_dram", (NB, P, 2, TILE), F32, kind="Internal").ap()
        w_dram = nc.dram_tensor("weights_dram", (LAYERS, P, WCOLS), F32, kind="Internal").ap()

        idb = sb("idb", [P, P], BF16)
        idf = sb("idf", [P, P], F32)
        zeros = sb("zeros", [P, 32], BF16)
        minus_half = sb("minus_half", [P, NS], F32)
        head_sel = sb("head_sel", [P, HEADS], F32)
        wts = sb("wts", [P, WCOLS], F32)
        k_t = sb("k_t", [P, HEADS, N], BF16)
        v_sb = sb("v_sb", [P, MT, HEADS, HD], F32)
        q_t = sb("q_t", [P, 2, NS, HEADS, P], BF16)
        q_a = sb("q_a", [KROWS, 2, HEADS, P], BF16)
        adj_in = sb("adj_in", [P, 2, CHUNK], I32)
        mask_n = sb("mask_n", [P, 2, CHUNK], BF16)
        arena = sb("arena", [P, 2 * MT, TILE], BF16)
        mask_t = arena
        p_buf = sb("p_buf", [P, 2, 4, TILE], F32)
        v_cur = sb("v_cur", [P, 2, HEADS, 32], F32)
        rmax = sb("rmax", [P, HEADS], F32)
        neg = sb("neg", [P, NS * HEADS], F32)
        neg_p = sb("neg_p", [P, NS, PARTS, HEADS], BF16)

        flat = arena[:].rearrange("p a b -> p (a b)")
        at = [0]

        def carve(cols, dt):
            width = 2 if dt == F32 else 1
            a = flat[:, at[0]:at[0] + cols * width]
            at[0] += cols * width
            return a.bitcast(F32) if dt == F32 else a

        xt = carve(NS * P, F32).rearrange("p (t c) -> p t c", t=NS)
        xn = carve(NS * P, F32).rearrange("p (t c) -> p t c", t=NS)
        xn_t = carve(TILE, F32)
        stats = carve(NS * 6, F32).rearrange("p (t c) -> p t c", t=NS)
        mv = carve(NS * 2, F32).rearrange("p (t c) -> p t c", t=NS)
        ve = carve(NS, F32)
        rstd = carve(NS, F32)
        parts = carve(NS * 2 * HEADS * (PARTS + 1) * HD, BF16).rearrange("p (g a d) -> p g a d", a=PARTS + 1, d=HD)
        rest = carve(NS * 2 * HEADS * HD, F32).rearrange("p (g d) -> p g d", d=HD)
        q_out = carve(NS * HEADS * P, BF16).rearrange("p (t h c) -> p t h c", t=NS, h=HEADS)
        o_in = carve(2 * TILE, F32).rearrange("p (a c) -> p a c", a=2)
        rsum = carve(NS * HEADS, F32)
        attn = carve(NS * P, F32)
        attn_t = carve(TILE, F32)
        x2 = carve(NS * P, F32)
        x3 = carve(NS * P, F32)
        g_t = carve(4 * TILE, F32).rearrange("p (f c) -> p f c", f=4)
        o_sb = sb("o_sb", [P, 2, TILE], F32)

        PS = ctx.enter_context(nc.psum_tensor("PS", [P, 8, TILE], F32))
        ps_b, ps_o, ps_a = PS[:, 0:4, :], PS[:, 4:6, :], PS[:, 6:8, :]

        w_loaded, w_packed, w_here = sem("w_loaded"), sem("w_packed"), sem("w_here")
        x_copied = sem("x_copied")
        set_up = sem("set_up")
        phase_end = sem("phase_end")
        seen = sem("seen")
        x_loaded, var_ready, rstd_ready = sem("x_loaded"), sem("var_ready"), sem("rstd_ready")
        xn_ready, xn_turned, xn_kept = sem("xn_ready"), sem("xn_turned"), sem("xn_kept")
        qkv_ready, v_kept, parts_ready = sem("qkv_ready"), sem("v_kept"), sem("parts_ready")
        qk_turned, qk_kept_act, qk_kept_dve, q_stored = (
            sem("qk_turned"), sem("qk_kept_act"), sem("qk_kept_dve"), sem("q_stored"))
        qt_loaded, qa_loaded = sem("qt_loaded"), sem("qa_loaded")
        adj_loaded = [sem("adj_loaded_0"), sem("adj_loaded_1")]
        mask_made, mask_turned, mask_kept = sem("mask_made"), sem("mask_turned"), sem("mask_kept")
        a_scored, a_maxed = sem("a_scored"), sem("a_maxed")
        neg_ready, neg_turned, neg_kept = sem("neg_ready"), sem("neg_turned"), sem("neg_kept")
        b_scored, b_exped, pv_done, v_set = sem("b_scored"), sem("b_exped"), sem("pv_done"), sem("v_set")
        o_kept_act, o_kept_dve, o_stored = sem("o_kept_act"), sem("o_kept_dve"), sem("o_stored")
        o_loaded, o_turned, attn_ready = sem("o_loaded"), sem("o_turned"), sem("attn_ready")
        attn_turned, attn_kept, proj_ready = sem("attn_turned"), sem("attn_kept"), sem("proj_ready")
        hid_ready, gelu_done, ff_ready, x3_ready, out_stored = (
            sem("hid_ready"), sem("gelu_done"), sem("ff_ready"), sem("x3_ready"), sem("out_stored"))

        A_BLOCKS = MB * HEADS
        B_PAIRS = STEPS * 4
        B_QUADS = STEPS * 2
        CREDIT_SCORED, CREDIT_MAXED = 2 * A_BLOCKS, 2
        CREDIT_MASK = 2
        CREDIT_EXPED, CREDIT_PV = 2, NS * B_QUADS

        def phase_barrier(eng, L, n):
            eng.drain().then_inc(phase_end, 1)
            eng.wait_ge(phase_end, (L * 3 + (n + 1)) * 5)
            eng.sem_inc(seen, 1)

        ring = []
        for mb in range(MB):
            for hs in range(2):
                if mb % 2 == 1 and hs == 0:
                    ring.append(("m", mb // 2))
                ring += [("a", mb * HEADS + 4 * hs + j) for j in range(4)]
        slot_of = {use: i % 2 for i, use in enumerate(ring)}
        before = {use: ring[i - 2] if i >= 2 else None for i, use in enumerate(ring)}
        assert len(ring) % 2 == 0

        def keep_turned(copy, g, i):
            bank = PS[0:KROWS, 6 + i % 2, :].bitcast(BF16)
            if i < 4:
                return copy(q_out[0:KROWS, :, 2 * i:2 * i + 2, :].rearrange("p t h c -> p h t c"),
                            bank.rearrange("p (h t c) -> p h t c", h=2, t=NS))
            return copy(k_t[0:KROWS, 2 * i - 8:2 * i - 6, bass.ds(g * TILE, TILE)],
                        bank.rearrange("p (h c) -> p h c", h=2))

        def keep_neg_half(copy, nb, half):
            src = ps_a[KROWS:KROWS + MROWS, 0, 0:TILE // 2].bitcast(BF16).rearrange("p (t a c) -> p t a c", t=NS, a=1)
            dst = q_t[KROWS:KROWS + MROWS, bass.ds(nb % 2, 1), :, 4 * half:4 * half + 4, :].rearrange("p a t h c -> p (a t) h c")
            return copy(dst, src.broadcast_to([MROWS, NS, 4, P]))

        block = ctx.enter_context(nc.Block())

        @block.sync
        def _(sp):
            for l in range(LAYERS):
                w = weights[l]
                wd = w_dram[l]
                col = lambda a: a.rearrange("(p a) -> p a", a=1)
                row = lambda a: a.rearrange("(a p) -> a p", a=1).broadcast_to([P, P])
                sp.dma_start(wd[:, C_QKV:C_PROJ], w["w_qkv"]).then_inc(w_packed, 16)
                sp.dma_start(wd[:, C_PROJ:C_W1], w["w_proj"]).then_inc(w_packed, 16)
                sp.dma_start(wd[:, C_W1:C_W2], w["w1"]).then_inc(w_packed, 16)
                sp.dma_start(wd[:, C_W2:C_BP].rearrange("p (f c) -> p f c", f=4),
                             w["w2"].rearrange("(f p) c -> p f c", p=P)).then_inc(w_packed, 16)
                sp.dma_start(wd[:, C_BP:C_B2], row(w["b_proj"])).then_inc(w_packed, 16)
                sp.dma_start(wd[:, C_B2:C_G1], row(w["b2"])).then_inc(w_packed, 16)
                sp.dma_start(wd[:, C_G1:C_G1 + 1], col(w["g1"]), allow_slow_non_contiguous=True).then_inc(w_packed, 16)
                sp.dma_start(wd[:, C_BE1:C_BE1 + 1], col(w["be1"]), allow_slow_non_contiguous=True).then_inc(w_packed, 16)
                sp.dma_start(wd[:, C_G2:C_G2 + 1], col(w["g2"]), allow_slow_non_contiguous=True).then_inc(w_packed, 16)
                sp.dma_start(wd[:, C_BE2:C_BE2 + 1], col(w["be2"]), allow_slow_non_contiguous=True).then_inc(w_packed, 16)
                sp.dma_start(wd[:, C_B1:C_B1 + 4], w["b1"].rearrange("(f p) -> p f", p=P),
                             allow_slow_non_contiguous=True).then_inc(w_packed, 16)
            sp.dma_start(out.rearrange("(a b) c -> a (b c)", a=P), x.rearrange("(a b) c -> a (b c)", a=P)).then_inc(x_copied, 16)
            sp.wait_ge(w_packed, 16 * 11 * LAYERS)
            sp.wait_ge(x_copied, 16)

            def x_rows(g):
                return out[bass.ds(g * TILE, TILE), :].rearrange("(t p) c -> p t c", p=P)

            with sp.Fori(0, LAYERS) as L:
                sp.dma_start(wts[:], w_dram[bass.ds(L, 1)].rearrange("a p c -> (a p) c")).then_inc(w_here, 16)
                with sp.Fori(0, NB) as g:
                    sp.wait_ge(xn_ready, (L * 2) * NB + g)
                    sp.dma_start(xt, x_rows(g)).then_inc(x_loaded, 16)
                    sp.wait_ge(qk_kept_act, (L * NB + g) * 4 + 2)
                    sp.wait_ge(qk_kept_dve, (L * NB + g) * 4 + 2)
                    sp.dma_start(q_dram[bass.ds(g, 1)].rearrange("a r t h c -> (a r) (t h c)"),
                                 q_out[0:KROWS].rearrange("p t h c -> p (t h c)")).then_inc(q_stored, 16)
                sp.wait_ge(q_stored, (L + 1) * NB * 16)
                sp.sem_inc(seen, 1)
                phase_barrier(sp, L, 0)

                with sp.Fori(0, NB) as nb:
                    sp.wait_ge(pv_done, (L * NB + nb) * (NS * B_QUADS))
                    sp.sem_inc(seen, 1)
                    sp.wait_ge(qt_loaded, (L * NB + nb) * 16)
                    sp.sem_inc(seen, 1)
                    sp.dma_start(q_t[0:KROWS, bass.ds(nb % 2, 1)].rearrange("p a t h c -> p (a t h c)"),
                                 q_dram[bass.ds(nb, 1)].rearrange("a r t h c -> (a r) (t h c)")).then_inc(qt_loaded, 16)
                    with sp.Fori(0, NS) as q:
                        ia = (L * NB + nb) * NS + q
                        sp.wait_ge(a_scored, ia * A_BLOCKS + (CREDIT_SCORED - A_BLOCKS))
                        sp.sem_inc(seen, 1)
                        sp.wait_ge(qa_loaded, ia * 16)
                        sp.dma_start(q_a[:, bass.ds(q % 2, 1)].rearrange("p a h c -> p (a h c)"),
                                     q_dram[bass.ds(nb, 1), :, bass.ds(q, 1)].rearrange("a r t h c -> (a r) (t h c)")).then_inc(qa_loaded, 16)
                        for c in range(NC):
                            sp.wait_ge(mask_made, ia * NC + (c - 1 + CREDIT_MASK))
                            sp.dma_start(adj_in[:, c % 2, :],
                                         adj[bass.ds(nb * TILE + q * P, P), c * CHUNK:(c + 1) * CHUNK]).then_inc(adj_loaded[c % 2], 16)
                phase_barrier(sp, L, 1)

                with sp.Fori(0, NB) as g:
                    sp.wait_ge(xn_ready, (L * 2 + 1) * NB + g)
                    sp.dma_start(xt, x_rows(g)).then_inc(x_loaded, 16)
                    sp.dma_start(o_in, o_dram[bass.ds(g, 1)].rearrange("a p b c -> (a p) b c")).then_inc(o_loaded, 16)
                    sp.wait_ge(x3_ready, L * NB + g + 1)
                    sp.dma_start(x_rows(g), x3.rearrange("p (t c) -> p t c", t=NS)).then_inc(out_stored, 16)
                sp.wait_ge(out_stored, (L + 1) * NB * 16)
                sp.sem_inc(seen, 1)
                phase_barrier(sp, L, 2)

        @block.tensor
        def _(pe):
            pe.sem_inc(a_scored, CREDIT_SCORED)
            pe.sem_inc(mask_turned, CREDIT_MASK)
            pe.sem_inc(pv_done, CREDIT_PV)
            pe.wait_ge(set_up, 5)

            def turn_normed(gx):
                pe.wait_ge(xn_ready, gx + 1)
                pe.wait_ge(xn_kept, gx)
                for t in range(NS):
                    mm = pe.transpose(PS[:, 0, t * P:(t + 1) * P], xn[:, t, :], idf[:])
                mm.then_inc(xn_turned, 1)

            def project(L):
                with pe.Fori(0, NB) as g:
                    gi, gx = L * NB + g, L * 2 * NB + g
                    turn_normed(gx)
                    pe.wait_ge(xn_kept, gx + 1)
                    pe.wait_ge(v_kept, gi)
                    pe.wait_ge(parts_ready, gi)
                    for t in range(NS):
                        mm = pe.matmul(PS[:, 1 + t, 0:384], xn_t[:, t * P:(t + 1) * P], wts[:, C_QKV:C_PROJ],
                                       start=True, stop=True)
                    mm.then_inc(qkv_ready, 1)
                    pe.wait_ge(parts_ready, gi + 1)
                    for i in range(HEADS):
                        kept = qk_kept_dve if i % 2 else qk_kept_act
                        pe.wait_ge(kept, gi * 4 + i // 2)
                        bank = PS[:, 6 + i % 2, :].bitcast(BF16)
                        for j in range(2):
                            hk = 2 * i + j
                            for r, first in enumerate(Q_PAIRS if hk < HEADS else K_PAIRS):
                                for t in range(NS):
                                    pair = parts[:, t * 2 * HEADS + hk, first:first + 2, :].rearrange("p a d -> p (a d)")
                                    mm = pe.transpose(bank[32 * r:32 * r + 32, (j * NS + t) * P:(j * NS + t + 1) * P],
                                                      pair, idb[:])
                        mm.then_inc(qk_turned, 1)

            def ring_slot(ia, use):
                last = before[use]
                if last is None:
                    n = {0: 2, 1: 1}[ring.index(use)]
                    pe.wait_ge(a_maxed, ia * A_BLOCKS + (1 - n + CREDIT_MAXED))
                elif last[0] == "a":
                    pe.wait_ge(a_maxed, ia * A_BLOCKS + (last[1] + 1 + CREDIT_MAXED))
                else:
                    pe.wait_ge(mask_kept, ia * NC + (last[1] + 1))
                return ps_a[:, slot_of[use], :]

            def score_a(ia, q, mb, h):
                k = mb * HEADS + h
                bank = ring_slot(ia, ("a", k))
                pe.matmul(bank, q_a[:, bass.ds(q % 2, 1), h, :].rearrange("p a c -> p (a c)"),
                          k_t[0:KROWS, h, mb * TILE:(mb + 1) * TILE], start=True, stop=True).then_inc(a_scored, 1)

            def turn_mask(ia, c):
                bank = ring_slot(ia, ("m", c)).bitcast(BF16)
                pe.wait_ge(mask_made, ia * NC + (c + 1 + CREDIT_MASK))
                for i in range(CHUNK // P):
                    mm = pe.transpose(bank[:, i * P:(i + 1) * P], mask_n[:, c % 2, i * P:(i + 1) * P], idb[:])
                mm.then_inc(mask_turned, 1)

            def score_b(ib, nb, q, s, k):
                pair = s * 4 + k
                pe.wait_ge(b_exped, ib * B_PAIRS + (pair - 1 + CREDIT_EXPED))
                for j in range(2):
                    h = 2 * k + j
                    bank = ps_b[:, 2 * (k % 2) + j, :]
                    pe.matmul(bank, k_t[0:KROWS + MROWS, h, bass.ds(q * (STEPS * P) + s * P, P)],
                              q_t[0:KROWS + MROWS, bass.ds(nb % 2, 1), :, h, :], start=True, stop=False)
                    mm = pe.matmul(bank, idb[:], mask_t[:, bass.ds((nb % 2) * MT + q * STEPS + s, 1), :].rearrange("p a c -> p (a c)"),
                                   start=False, stop=True)
                mm.then_inc(b_scored, 1)

            def gather_v(ib, s, quad):
                t = 2 * s + quad
                pe.wait_ge(b_exped, ib * B_PAIRS + (2 * t + 2 + CREDIT_EXPED))
                if quad == 0:
                    pe.wait_ge(v_set, ib * STEPS + (s + 1))
                for j in range(4):
                    mm = pe.matmul(ps_o[32 * j:32 * j + 32, quad, :], v_cur[:, s % 2, 4 * quad + j, :],
                                   p_buf[:, quad, j, :], start=False, stop=False, skip_group_check=True)
                mm.then_inc(pv_done, 1)

            def body(ia, ib, nb, q, a, b):
                if a:
                    pe.wait_ge(qa_loaded, ia * 16 + 16)
                for s in range(STEPS):
                    for quad in range(2):
                        last = s == STEPS - 1 and quad == 1
                        if a and quad == 0 and s % 2 == 1:
                            turn_mask(ia, s // 2)
                        heads = [4 * quad + j for j in range(4)]
                        if not b:
                            for h in heads:
                                score_a(ia, q, s, h)
                            continue
                        if a and not last:
                            score_a(ia, q, s, heads[0])
                        score_b(ib, nb, q, s, 2 * quad)
                        if a and not last:
                            score_a(ia, q, s, heads[1])
                        score_b(ib, nb, q, s, 2 * quad + 1)
                        if a and not last:
                            score_a(ia, q, s, heads[2])
                            score_a(ia, q, s, heads[3])
                        if 2 * s + quad > 0:
                            gather_v(ib, (2 * s + quad - 1) // 2, (quad + 1) % 2)
                        if a and last:
                            for h in heads:
                                score_a(ia, q, s, h)
                if b:
                    gather_v(ib, STEPS - 1, 1)

            def turn_neg(ja):
                pe.wait_ge(neg_ready, ja + 1)
                bank = ps_a[:, 0, :].bitcast(BF16)
                for t in range(NS):
                    mm = pe.transpose(bank[KROWS:KROWS + MROWS, t * P:(t + 1) * P],
                                      neg_p[:, t, :, :].rearrange("p a h -> p (a h)"), idb[:])
                mm.then_inc(neg_turned, 1)

            def start_b(jb):
                pe.wait_ge(qt_loaded, jb * 16 + 16)
                pe.wait_ge(neg_kept, jb * 2 + 2)
                pe.wait_ge(mask_kept, jb * NS * NC + NS * NC)
                pe.wait_ge(o_kept_act, jb)
                pe.wait_ge(o_kept_dve, jb)
                for h in range(HEADS):
                    j = h % 4
                    pe.matmul(ps_o[32 * j:32 * j + 32, h // 4, :], zeros[:], k_t[:, 0, 0:TILE],
                              start=True, stop=False, skip_group_check=True)

            def attend(L):
                with pe.Fori(0, NS) as q:
                    body(L * NB * NS + q, None, None, q, True, False)
                turn_neg(L * NB)
                with pe.Fori(0, NB - 1) as nb:
                    start_b(L * NB + nb)
                    with pe.Fori(0, NS) as q:
                        ib = (L * NB + nb) * NS + q
                        body(ib + NS, ib, nb, q, True, True)
                    turn_neg(L * NB + nb + 1)
                start_b(L * NB + (NB - 1))
                with pe.Fori(0, NS) as q:
                    body(None, (L * NB + (NB - 1)) * NS + q, NB - 1, q, False, True)

            def feed_forward(L):
                with pe.Fori(0, NB) as g:
                    gi, gx = L * NB + g, (L * 2 + 1) * NB + g
                    pe.wait_ge(o_loaded, gi * 16 + 16)
                    pe.wait_ge(attn_ready, gi)
                    for t in range(NS):
                        for half in range(2):
                            i = 2 * t + half
                            mm = pe.transpose(PS[:, i // 4, (i % 4) * P:(i % 4 + 1) * P],
                                              o_in[:, half, t * P:(t + 1) * P], idf[:])
                    mm.then_inc(o_turned, 1)
                    pe.wait_ge(attn_ready, gi + 1)
                    for t in range(NS):
                        mm = pe.transpose(PS[:, 2, t * P:(t + 1) * P], attn[:, t * P:(t + 1) * P], idf[:])
                    mm.then_inc(attn_turned, 1)
                    pe.wait_ge(attn_kept, gi + 1)
                    pe.wait_ge(x3_ready, gi)
                    for t in range(NS):
                        mm = pe.matmul(PS[:, 3, t * P:(t + 1) * P], attn_t[:, t * P:(t + 1) * P],
                                       wts[:, C_PROJ:C_W1], start=True, stop=True)
                    mm.then_inc(proj_ready, 1)
                    turn_normed(gx)
                    pe.wait_ge(xn_kept, gx + 1)
                    pe.wait_ge(gelu_done, gi * 4)
                    for f in range(4):
                        pe.matmul(PS[:, 4 + f, :], wts[:, C_W1 + f * P:C_W1 + (f + 1) * P], xn_t,
                                  start=True, stop=True).then_inc(hid_ready, 1)
                    pe.wait_ge(gelu_done, gi * 4 + 4)
                    for t in range(NS):
                        for f in range(4):
                            mm = pe.matmul(PS[:, 3, t * P:(t + 1) * P], g_t[:, f, t * P:(t + 1) * P],
                                           wts[:, C_W2 + f * P:C_W2 + (f + 1) * P], start=f == 0, stop=f == 3)
                    mm.then_inc(ff_ready, 1)

            with pe.Fori(0, LAYERS) as L:
                pe.wait_ge(w_here, L * 16 + 16)
                pe.sem_inc(seen, 1)
                project(L)
                phase_barrier(pe, L, 0)
                attend(L)
                phase_barrier(pe, L, 1)
                feed_forward(L)
                phase_barrier(pe, L, 2)

        @block.scalar
        def _(act):
            act.sem_inc(b_exped, CREDIT_EXPED)
            act.dma_start(idb[:], ident).then_inc(w_loaded, 16)
            act.dma_start(idf[:], ident_f).then_inc(w_loaded, 16)
            act.dma_start(head_sel[KROWS:P, :], head_rows).then_inc(w_loaded, 16)
            act.wait_ge(w_loaded, 48)
            act.drain().then_inc(set_up, 1)

            def keep_normed(gx, scale_col, bias_col):
                act.wait_ge(xn_turned, gx + 1)
                nc.scalar.activation(xn_t, PS[:, 0, :], ACT.Identity, bias=wts[:, bias_col:bias_col + 1],
                                     scale=wts[:, scale_col:scale_col + 1]).then_inc(xn_kept, 1)

            def project(L):
                with act.Fori(0, NB) as g:
                    gi, gx = L * NB + g, L * 2 * NB + g
                    act.wait_ge(qkv_ready, gi)
                    keep_normed(gx, C_G1, C_BE1)
                    act.wait_ge(qkv_ready, gi + 1)
                    nc.scalar.activation(v_sb[:, bass.ds(g * NS, NS)].rearrange("p t h d -> p t (h d)"),
                                         PS[:, 1:5, 256:384], ACT.Copy).then_inc(v_kept, 1)
                    act.wait_ge(q_stored, gi * 16)
                    for i in range(0, HEADS, 2):
                        act.wait_ge(qk_turned, gi * 8 + (i + 1))
                        keep_turned(nc.scalar.copy, g, i).then_inc(qk_kept_act, 1)

            def exp_pair(ib, pair):
                quad = pair // 2
                act.wait_ge(b_scored, ib * B_PAIRS + (pair + 1))
                if pair % 2 == 0:
                    act.wait_ge(pv_done, ib * B_QUADS + (quad - 1 + CREDIT_PV))
                j = 2 * (pair % 2)
                nc.scalar.activation(p_buf[:, quad % 2, j:j + 2, :], ps_b[:, j:j + 2, :],
                                     ACT.Exp, scale=SCALE).then_inc(b_exped, 1)

            def keep_mask(ia, nb, q, c):
                act.wait_ge(mask_turned, ia * NC + (c + 1 + CREDIT_MASK))
                n = CHUNK // P
                nc.scalar.activation(mask_t[:, bass.ds((nb % 2) * MT + c * n, n), bass.ds(q * P, P)],
                                     ps_a[:, slot_of[("m", c)], :].bitcast(BF16).rearrange("p (m c) -> p m c", m=n),
                                     ACT.Copy).then_inc(mask_kept, 1)

            def body(ia, ib, nba, q, a, b):
                for s in range(STEPS):
                    for k in range(4):
                        if b:
                            exp_pair(ib, 4 * s + k)
                        if a and s % 2 == 1 and k == 0:
                            keep_mask(ia, nba, q, s // 2)

            def keep_neg(ja, nb):
                act.wait_ge(neg_turned, ja + 1)
                keep_neg_half(nc.scalar.copy, nb, 0).then_inc(neg_kept, 1)

            def store_o(jb, nb):
                act.wait_ge(pv_done, jb * (NS * B_QUADS) + (NS * B_QUADS + CREDIT_PV))
                act.wait_ge(o_stored, jb * 16)
                nc.scalar.copy(o_sb[:, 0, :], ps_o[:, 0, :]).then_inc(o_kept_act, 1)
                act.wait_ge(o_kept_act, jb + 1)
                act.wait_ge(o_kept_dve, jb + 1)
                act.dma_start(o_dram[bass.ds(nb, 1)].rearrange("a p b c -> (a p) (b c)"),
                              o_sb[:].rearrange("p b c -> p (b c)")).then_inc(o_stored, 16)

            def attend(L):
                with act.Fori(0, NS) as q:
                    body(L * NB * NS + q, None, 0, q, True, False)
                keep_neg(L * NB, 0)
                with act.Fori(0, NB - 1) as nb:
                    with act.Fori(0, NS) as q:
                        ib = (L * NB + nb) * NS + q
                        body(ib + NS, ib, nb + 1, q, True, True)
                    store_o(L * NB + nb, nb)
                    keep_neg(L * NB + nb + 1, nb + 1)
                with act.Fori(0, NS) as q:
                    body(None, (L * NB + (NB - 1)) * NS + q, None, q, False, True)
                store_o(L * NB + (NB - 1), NB - 1)
                act.wait_ge(o_stored, (L + 1) * NB * 16)
                act.sem_inc(seen, 1)

            def feed_forward(L):
                with act.Fori(0, NB) as g:
                    gi, gx = L * NB + g, (L * 2 + 1) * NB + g
                    act.wait_ge(attn_turned, gi + 1)
                    act.wait_ge(proj_ready, gi)
                    nc.scalar.copy(attn_t, PS[:, 2, :]).then_inc(attn_kept, 1)
                    act.wait_ge(hid_ready, gi * 4)
                    keep_normed(gx, C_G2, C_BE2)
                    act.wait_ge(ff_ready, gi)
                    for f in range(4):
                        act.wait_ge(hid_ready, gi * 4 + (f + 1))
                        nc.scalar.activation(g_t[:, f, :], PS[:, 4 + f, :], ACT.Gelu_apprx_tanh,
                                             bias=wts[:, C_B1 + f:C_B1 + f + 1]).then_inc(gelu_done, 1)

            with act.Fori(0, LAYERS) as L:
                act.wait_ge(w_here, L * 16 + 16)
                project(L)
                phase_barrier(act, L, 0)
                attend(L)
                phase_barrier(act, L, 1)
                feed_forward(L)
                phase_barrier(act, L, 2)

        @block.vector
        def _(dve):
            dve.sem_inc(a_maxed, CREDIT_MAXED)
            dve.sem_inc(mask_made, CREDIT_MASK)

            def until(s, value):
                dve.wait_ge(s, value)
                dve.sem_inc(seen, 1)

            dve.memset(zeros[:], 0.0)
            dve.memset(minus_half[:], -0.5)
            dve.memset(v_cur[:], 0.0)
            dve.drain()
            dve.memset(v_cur[:, :, :, HD:HD + 1], 1.0)
            dve.memset(k_t[KROWS:P, :, :], 1.0)
            dve.drain()
            dve.wait_ge(w_loaded, 48)
            for h in range(HEADS):
                dve.tensor_scalar(k_t[KROWS:P, h, :], k_t[KROWS:P, h, :], head_sel[KROWS:P, h:h + 1], None, ALU.mult)
            dve.drain().then_inc(set_up, 4)

            def norm(src, gx):
                for t in range(NS):
                    dve.bn_stats(stats[:, t, :], src[:, t, :])
                dve.drain()
                for t in range(NS):
                    last = dve.bn_aggr(mv[:, t, :], stats[:, t, :])
                last.then_inc(var_ready, 1)
                until(rstd_ready, gx + 1)
                until(xn_turned, gx)
                for t in range(NS):
                    last = dve.tensor_scalar(xn[:, t, :], src[:, t, :], mv[:, t, 0:1], rstd[:, t:t + 1],
                                             ALU.subtract, ALU.mult)
                last.then_inc(xn_ready, 1)

            def project(L):
                with dve.Fori(0, NB) as g:
                    gi, gx = L * NB + g, L * 2 * NB + g
                    until(x_loaded, gx * 16 + 16)
                    norm(xt, gx)
                    until(v_kept, gi + 1)
                    until(qk_turned, gi * 8)
                    qk = PS[:, 1:5, 0:256].rearrange("p t (g d) -> p t g d", d=HD)
                    p4 = parts.rearrange("p (t g) a d -> p t g a d", t=NS)
                    r4 = rest.rearrange("p (t g) d -> p t g d", t=NS)
                    dve.tensor_copy(p4[:, :, :, 0, :], qk)
                    dve.drain()
                    dve.tensor_tensor(r4, qk, p4[:, :, :, 0, :], ALU.subtract)
                    dve.tensor_copy(parts[:, :, 1, :], parts[:, :, 0, :])
                    dve.drain()
                    dve.tensor_copy(parts[:, :, 2, :], rest)
                    dve.drain()
                    dve.tensor_tensor(parts[:, :, 3, :], rest, parts[:, :, 2, :], ALU.subtract).then_inc(parts_ready, 1)
                    until(q_stored, gi * 16)
                    for i in range(1, HEADS, 2):
                        until(qk_turned, gi * 8 + (i + 1))
                        keep_turned(dve.tensor_copy, g, i).then_inc(qk_kept_dve, 1)

            def body(ia, q):
                for mb in range(MB):
                    c = mb // 2
                    if mb % 2 == 0:
                        until(adj_loaded[c % 2], ia * (NC // 2 * 16) + (c // 2 + 1) * 16)
                        until(mask_turned, ia * NC + (c - 1 + CREDIT_MASK))
                        until(a_maxed, ia * A_BLOCKS + (2 * HEADS * (c - 1) + CREDIT_MAXED if c else 0))
                        dve.tensor_scalar(mask_n[:, c % 2, :], adj_in[:, c % 2, :], 0.0, MASKED,
                                          ALU.is_equal, ALU.mult).then_inc(mask_made, 1)
                        until(mask_made, ia * NC + (c + 1 + CREDIT_MASK))
                    for h in range(HEADS):
                        k = mb * HEADS + h
                        if mb and h % 4 == 0:
                            until(a_maxed, ia * A_BLOCKS + (k - 4 + CREDIT_MAXED))
                        if not mb and h == 0:
                            until(neg_ready, 0)
                        until(a_scored, ia * A_BLOCKS + (k + 1 + CREDIT_SCORED))
                        first = LOWEST if mb == 0 else rmax[:, h:h + 1]
                        bank = ps_a[:, slot_of[("a", k)], :]
                        dve.tensor_tensor_reduce(bank, bank,
                                                 mask_n[:, c % 2, (mb % 2) * TILE:(mb % 2 + 1) * TILE],
                                                 1.0, first, ALU.add, ALU.max, rmax[:, h:h + 1]).then_inc(a_maxed, 1)
                until(a_maxed, ia * A_BLOCKS + (A_BLOCKS + CREDIT_MAXED))
                dve.tensor_scalar(neg[:, bass.ds(q * HEADS, HEADS)], rmax[:], -1.0, None, ALU.mult)
                dve.drain()

            def split_neg(ja, nb):
                n3 = neg[:].rearrange("p (t h) -> p t h", t=NS)
                until(neg_turned, ja)
                dve.tensor_copy(neg_p[:, :, 0, :], n3)
                dve.drain()
                dve.tensor_tensor(n3, n3, neg_p[:, :, 0, :], ALU.subtract)
                dve.drain()
                dve.tensor_copy(neg_p[:, :, 1, :], n3)
                dve.drain()
                dve.tensor_tensor(neg_p[:, :, 2, :], n3, neg_p[:, :, 1, :], ALU.subtract).then_inc(neg_ready, 1)

            def keep_neg(ja, nb):
                until(neg_kept, ja * 2 + 1)
                keep_neg_half(dve.tensor_copy, nb, 1).then_inc(neg_kept, 1)

            def keep_o(jb):
                until(pv_done, jb * (NS * B_QUADS) + (NS * B_QUADS + CREDIT_PV))
                until(o_stored, jb * 16)
                dve.tensor_copy(o_sb[:, 1, :], ps_o[:, 1, :]).then_inc(o_kept_dve, 1)

            def attend(L):
                with dve.Fori(0, NS) as q:
                    body(L * NB * NS + q, q)
                split_neg(L * NB, 0)
                keep_neg(L * NB, 0)
                with dve.Fori(0, NB - 1) as nb:
                    with dve.Fori(0, NS) as q:
                        body((L * NB + nb + 1) * NS + q, q)
                    split_neg(L * NB + nb + 1, nb + 1)
                    keep_o(L * NB + nb)
                    keep_neg(L * NB + nb + 1, nb + 1)
                keep_o(L * NB + (NB - 1))

            def feed_forward(L):
                with dve.Fori(0, NB) as g:
                    gi, gx = L * NB + g, (L * 2 + 1) * NB + g
                    until(o_turned, gi + 1)
                    rows = PS[:, 0:2, :].rearrange("p b (g d) -> p (b g) d", d=32)
                    sums = rsum.rearrange("p (g d) -> p g d", d=1)
                    dve.reciprocal(sums, rows[:, :, HD:HD + 1])
                    dve.drain()
                    until(attn_turned, gi)
                    dve.tensor_tensor(attn.rearrange("p (g d) -> p g d", d=HD), rows[:, :, 0:HD],
                                      sums.broadcast_to([P, NS * HEADS, HD]), ALU.mult).then_inc(attn_ready, 1)
                    until(x_loaded, gx * 16 + 16)
                    bp = wts[:, C_BP:C_B2].rearrange("p (a c) -> p a c", a=1).broadcast_to([P, NS, P])
                    b2 = wts[:, C_B2:C_G1].rearrange("p (a c) -> p a c", a=1).broadcast_to([P, NS, P])
                    x2v = x2.rearrange("p (t c) -> p t c", t=NS)
                    dve.tensor_tensor(x2v, xt, bp, ALU.add)
                    dve.drain()
                    until(proj_ready, gi + 1)
                    dve.tensor_tensor(x2, PS[:, 3, :], x2, ALU.add)
                    dve.drain()
                    norm(x2v, gx)
                    dve.drain()
                    dve.tensor_tensor(x2v, x2v, b2, ALU.add)
                    dve.drain()
                    until(ff_ready, gi + 1)
                    until(out_stored, gi * 16)
                    dve.tensor_tensor(x3, PS[:, 3, :], x2, ALU.add).then_inc(x3_ready, 1)

            with dve.Fori(0, LAYERS) as L:
                until(w_here, L * 16 + 16)
                project(L)
                phase_barrier(dve, L, 0)
                attend(L)
                phase_barrier(dve, L, 1)
                feed_forward(L)
                phase_barrier(dve, L, 2)

        @block.gpsimd
        def _(pool):
            pool.wait_ge(set_up, 5)

            def rstds(gx0):
                with pool.Fori(0, NB) as g:
                    pool.wait_ge(var_ready, gx0 + g + 1)
                    pool.sem_inc(seen, 1)
                    pool.tensor_scalar(ve, mv[:, :, 1], EPS, None, ALU.add)
                    pool.drain()
                    pool.tensor_tensor(rstd, ve, minus_half[:], ALU.pow).then_inc(rstd_ready, 1)

            def values(L):
                with pool.Fori(0, NB) as nb:
                    with pool.Fori(0, NS) as q:
                        ib = (L * NB + nb) * NS + q
                        for s in range(STEPS):
                            pool.wait_ge(pv_done, ib * B_QUADS + (2 * s - 2 + CREDIT_PV))
                            pool.tensor_copy(v_cur[:, s % 2, :, 0:HD],
                                             v_sb[:, bass.ds(q * STEPS + s, 1), :, :].rearrange("p a h d -> p (a h) d")).then_inc(v_set, 1)

            with pool.Fori(0, LAYERS) as L:
                rstds(L * 2 * NB)
                phase_barrier(pool, L, 0)
                values(L)
                phase_barrier(pool, L, 1)
                rstds((L * 2 + 1) * NB)
                phase_barrier(pool, L, 2)


def kernel(**inputs):
    import numpy as np
    import ml_dtypes
    import concourse.bacc as bacc
    from concourse.bass_utils import run_bass_kernel_spmd

    nc = bacc.Bacc("TRN2", target_bir_lowering=False, num_devices=1)
    arrays, aps = {}, {}

    def give(name, a):
        a = np.ascontiguousarray(a)
        arrays[f"in_{name}"] = a
        aps[name] = nc.dram_tensor(f"in_{name}", a.shape, mybir.dt.from_np(a.dtype), kind="ExternalInput").ap()
        return aps[name]

    give("x", inputs["x"])
    give("adj", inputs["adj"])
    weights = [{n: give(f"L{l}_gnn_{n}", inputs[f"L{l}_gnn_{n}"]) for n in NAMES} for l in range(LAYERS)]
    ident = give("ident", np.eye(P, dtype=ml_dtypes.bfloat16))
    ident_f = give("ident_f", np.eye(P, dtype=np.float32))
    rows = np.zeros((P - KROWS, HEADS), np.float32)
    for i in range(MROWS):
        rows[i, i % HEADS] = 1.0
    head_rows = give("head_rows", rows)
    out = nc.dram_tensor("out_dram", (N, P), F32, kind="ExternalOutput").ap()
    gnn_kernel(nc, aps["x"], aps["adj"], weights, ident, ident_f, head_rows, out)
    r = run_bass_kernel_spmd(nc, [arrays], core_ids=[0])
    return r.results[0]["out_dram"]
```

```python
from contextlib import ExitStack

import concourse.bass as bass
from concourse import mybir

ALU = mybir.AluOpType
ACT = mybir.ActivationFunctionType
F32 = mybir.dt.float32
BF16 = mybir.dt.bfloat16
I32 = mybir.dt.int32

P = 128
N = 4096
HEADS, HD = 8, 16
FF = 512
LAYERS = 2
EPS = 1e-5
SCALE = HD ** -0.5

TILE = 512
NB = N // TILE
NS = TILE // P
MT = N // P
MB = N // TILE
STEPS = MT // NS
CHUNK = 1024
NC = N // CHUNK
PARTS = 3
KROWS = 2 * PARTS * HD
MROWS = PARTS * HEADS
MASKED = -(2.0 ** 100)
LOWEST = -3e38
SPILLS = 2
P_SLOTS = 4
LAG = 2
POOL_OPS = ((0, 2), (2, 1), (4, 2))
POOL_HEADS = [h + i for h, n in POOL_OPS for i in range(n)]

Q_PAIRS = (1, 0, 2)
K_PAIRS = (1, 2, 0)

C_QKV, C_PROJ, C_W1, C_W2 = 0, 384, 512, 1024
C_BP, C_B2, C_G1 = 1536, 1664, 1792
C_BE1, C_G2, C_BE2, C_B1 = 1793, 1794, 1795, 1796
WCOLS = 1800

NAMES = ("w_qkv", "w_proj", "b_proj", "w1", "b1", "w2", "b2", "g1", "be1", "g2", "be2")


def gnn_kernel(nc, x, adj, weights, ident, ident_f, head_rows, out):
    ctx = ExitStack()
    with ctx:
        def sb(name, shape, dt):
            return ctx.enter_context(nc.sbuf_tensor(name, shape, dt))

        def sem(name):
            return ctx.enter_context(nc.semaphore(name))

        q_dram = nc.dram_tensor("q_parts_dram", (NB, KROWS, NS, HEADS, P), BF16, kind="Internal").ap()
        o_dram = nc.dram_tensor("attn_dram", (NB, P, 2, TILE), F32, kind="Internal").ap()
        w_dram = nc.dram_tensor("weights_dram", (LAYERS, P, WCOLS), F32, kind="Internal").ap()

        idb = sb("idb", [P, P], BF16)
        idf = sb("idf", [P, P], F32)
        zeros = sb("zeros", [P, 32], BF16)
        minus_half = sb("minus_half", [P, NS], F32)
        head_sel = sb("head_sel", [P, HEADS], F32)
        k_t = sb("k_t", [P, HEADS, N], BF16)
        v_sb = sb("v_sb", [P, MT, HEADS, HD], F32)
        q_t = sb("q_t", [P, 2, NS, HEADS, P], BF16)
        q_a = sb("q_a", [KROWS, 2, HEADS, P], BF16)
        adj_in = sb("adj_in", [P, 2, CHUNK], I32)
        mask_n = sb("mask_n", [P, 2, CHUNK], BF16)
        arena = sb("arena", [P, 2 * MT, TILE], BF16)
        mask_t = arena
        p_buf = sb("p_buf", [P, P_SLOTS, 4, TILE], F32)
        mask01 = sb("mask01", [P, 2, TILE], I32)
        spill = sb("spill", [P, SPILLS, TILE], BF16)
        v_cur = sb("v_cur", [P, 2, HEADS, 32], F32)
        rmax = sb("rmax", [P, HEADS], F32)
        rlast = sb("rlast", [P, HEADS], F32)
        neg = sb("neg", [P, (NS + 1) * HEADS], F32)
        neg_p = sb("neg_p", [P, NS, PARTS, HEADS], BF16)

        flat = arena[:].rearrange("p a b -> p (a b)")
        at = [0]

        def carve(cols, dt):
            width = 2 if dt == F32 else 1
            a = flat[:, at[0]:at[0] + cols * width]
            at[0] += cols * width
            return a.bitcast(F32) if dt == F32 else a

        wts = carve(WCOLS, F32)
        xt = carve(NS * P, F32).rearrange("p (t c) -> p t c", t=NS)
        xn = carve(NS * P, F32).rearrange("p (t c) -> p t c", t=NS)
        xn_t = carve(TILE, F32)
        stats = carve(NS * 6, F32).rearrange("p (t c) -> p t c", t=NS)
        mv = carve(NS * 2, F32).rearrange("p (t c) -> p t c", t=NS)
        ve = carve(NS, F32)
        rstd = carve(NS, F32)
        parts = carve(NS * 2 * HEADS * (PARTS + 1) * HD, BF16).rearrange("p (g a d) -> p g a d", a=PARTS + 1, d=HD)
        rest = carve(NS * 2 * HEADS * HD, F32).rearrange("p (g d) -> p g d", d=HD)
        q_out = carve(NS * HEADS * P, BF16).rearrange("p (t h c) -> p t h c", t=NS, h=HEADS)
        o_in = carve(2 * TILE, F32).rearrange("p (a c) -> p a c", a=2)
        rsum = carve(NS * HEADS, F32)
        attn = carve(NS * P, F32)
        attn_t = carve(TILE, F32)
        x2 = carve(NS * P, F32)
        x3 = carve(NS * P, F32)
        g_t = carve(4 * TILE, F32).rearrange("p (f c) -> p f c", f=4)
        o_sb = sb("o_sb", [P, 2, TILE], F32)

        PS = ctx.enter_context(nc.psum_tensor("PS", [P, 8, TILE], F32))
        ps_b, ps_o, ps_a = PS[:, 0:4, :], PS[:, 4:6, :], PS[:, 6:8, :]

        w_loaded, w_packed, w_here = sem("w_loaded"), sem("w_packed"), sem("w_here")
        x_copied = sem("x_copied")
        set_up = sem("set_up")
        phase_end = sem("phase_end")
        seen = sem("seen")
        x_loaded, var_ready, rstd_ready = sem("x_loaded"), sem("var_ready"), sem("rstd_ready")
        xn_ready, xn_turned, xn_kept = sem("xn_ready"), sem("xn_turned"), sem("xn_kept")
        qkv_ready, v_kept, parts_ready = sem("qkv_ready"), sem("v_kept"), sem("parts_ready")
        qk_turned, qk_kept_act, qk_kept_dve, q_stored = (
            sem("qk_turned"), sem("qk_kept_act"), sem("qk_kept_dve"), sem("q_stored"))
        qt_loaded, qa_loaded = sem("qt_loaded"), sem("qa_loaded")
        adj_loaded = [sem("adj_loaded_0"), sem("adj_loaded_1")]
        mask_made, mask_turned, mask_kept = sem("mask_made"), sem("mask_turned"), sem("mask_kept")
        a_scored, a_maxed = sem("a_scored"), sem("a_maxed")
        neg_set = sem("neg_set")
        neg_ready, neg_turned, neg_kept = sem("neg_ready"), sem("neg_turned"), sem("neg_kept")
        b_scored, b_exped, pv_done, v_set = sem("b_scored"), sem("b_exped"), sem("pv_done"), sem("v_set")
        mask01_made, p_masked = sem("mask01_made"), sem("p_masked")
        o_kept_act, o_kept_dve, o_stored = sem("o_kept_act"), sem("o_kept_dve"), sem("o_stored")
        o_loaded, o_turned, attn_ready = sem("o_loaded"), sem("o_turned"), sem("attn_ready")
        attn_turned, attn_kept, proj_ready = sem("attn_turned"), sem("attn_kept"), sem("proj_ready")
        hid_ready, gelu_done, ff_ready, x3_ready, out_stored = (
            sem("hid_ready"), sem("gelu_done"), sem("ff_ready"), sem("x3_ready"), sem("out_stored"))

        A_BLOCKS = MB * HEADS
        B_PAIRS = STEPS * 4
        B_QUADS = STEPS * 2
        CREDIT_SCORED, CREDIT_MAXED = 2 * A_BLOCKS, 3
        CREDIT_MASK = 2
        CREDIT_EXPED, CREDIT_PV, CREDIT_KEPT = 2, NS * B_QUADS + 1, 2
        B_MASKS = STEPS - 1
        B_POOLED = B_MASKS * len(POOL_OPS)
        ONE = 1
        from_one = {
            "sp": (q_stored, qt_loaded, qa_loaded, out_stored),
            "pool": (p_masked,),
            "pe": (qkv_ready, qk_turned, xn_turned, neg_turned, proj_ready, hid_ready, ff_ready, attn_turned),
            "act": (xn_kept, v_kept, qk_kept_act, o_kept_act, o_stored, gelu_done),
            "dve": (neg_set, xn_ready, parts_ready, qk_kept_dve, o_kept_dve, attn_ready, x3_ready),
        }

        def phase_barrier(eng, L, n):
            eng.drain().then_inc(phase_end, 1)
            eng.wait_ge(phase_end, (L * 3 + (n + 1)) * 5)
            eng.sem_inc(seen, 1)

        ring = []
        for step in range(STEPS):
            ring += [("b", 4 * step), ("b", 4 * step + 1)]
            if step % 2 == 1:
                ring.append(("m", step // 2))
            ring += [("b", 4 * step + 2), ("b", 4 * step + 3)]
        assert len(ring) % 2 == 0
        slot_of = {use: i % 2 for i, use in enumerate(ring)}

        def slot_before(use, a, b):
            there = [u for u in ring if slot_of[u] == slot_of[use] and (b if u[0] == "b" else a)]
            i = there.index(use)
            return there[i - 1], i == 0

        def keep_turned(copy, g, i):
            bank = PS[0:KROWS, 6 + i % 2, :].bitcast(BF16)
            if i < 4:
                return copy(q_out[0:KROWS, :, 2 * i:2 * i + 2, :].rearrange("p t h c -> p h t c"),
                            bank.rearrange("p (h t c) -> p h t c", h=2, t=NS))
            return copy(k_t[0:KROWS, 2 * i - 8:2 * i - 6, bass.ds(g * TILE, TILE)],
                        bank.rearrange("p (h c) -> p h c", h=2))

        def keep_neg_half(copy, nb, half):
            src = ps_a[KROWS:KROWS + MROWS, 0, 0:TILE // 2].bitcast(BF16).rearrange("p (t a c) -> p t a c", t=NS, a=1)
            dst = q_t[KROWS:KROWS + MROWS, bass.ds(nb % 2, 1), :, 4 * half:4 * half + 4, :].rearrange("p a t h c -> p (a t) h c")
            return copy(dst, src.broadcast_to([MROWS, NS, 4, P]))

        block = ctx.enter_context(nc.Block())

        @block.sync
        def _(sp):
            for s in from_one["sp"]:
                sp.sem_inc(s, ONE)
            for l in range(LAYERS):
                w = weights[l]
                wd = w_dram[l]
                col = lambda a: a.rearrange("(p a) -> p a", a=1)
                row = lambda a: a.rearrange("(a p) -> a p", a=1).broadcast_to([P, P])
                sp.dma_start(wd[:, C_QKV:C_PROJ], w["w_qkv"]).then_inc(w_packed, 16)
                sp.dma_start(wd[:, C_PROJ:C_W1], w["w_proj"]).then_inc(w_packed, 16)
                sp.dma_start(wd[:, C_W1:C_W2], w["w1"]).then_inc(w_packed, 16)
                sp.dma_start(wd[:, C_W2:C_BP].rearrange("p (f c) -> p f c", f=4),
                             w["w2"].rearrange("(f p) c -> p f c", p=P)).then_inc(w_packed, 16)
                sp.dma_start(wd[:, C_BP:C_B2], row(w["b_proj"])).then_inc(w_packed, 16)
                sp.dma_start(wd[:, C_B2:C_G1], row(w["b2"])).then_inc(w_packed, 16)
                sp.dma_start(wd[:, C_G1:C_G1 + 1], col(w["g1"]), allow_slow_non_contiguous=True).then_inc(w_packed, 16)
                sp.dma_start(wd[:, C_BE1:C_BE1 + 1], col(w["be1"]), allow_slow_non_contiguous=True).then_inc(w_packed, 16)
                sp.dma_start(wd[:, C_G2:C_G2 + 1], col(w["g2"]), allow_slow_non_contiguous=True).then_inc(w_packed, 16)
                sp.dma_start(wd[:, C_BE2:C_BE2 + 1], col(w["be2"]), allow_slow_non_contiguous=True).then_inc(w_packed, 16)
                sp.dma_start(wd[:, C_B1:C_B1 + 4], w["b1"].rearrange("(f p) -> p f", p=P),
                             allow_slow_non_contiguous=True).then_inc(w_packed, 16)
            sp.dma_start(out.rearrange("(a b) c -> a (b c)", a=P), x.rearrange("(a b) c -> a (b c)", a=P)).then_inc(x_copied, 16)
            sp.wait_ge(w_packed, 16 * 11 * LAYERS)
            sp.wait_ge(x_copied, 16)

            def x_rows(g):
                return out[bass.ds(g * TILE, TILE), :].rearrange("(t p) c -> p t c", p=P)

            with sp.Fori(0, LAYERS) as L:
                sp.dma_start(wts, w_dram[bass.ds(L, 1)].rearrange("a p c -> (a p) c")).then_inc(w_here, 16)
                with sp.Fori(0, NB) as g:
                    sp.wait_ge(xn_ready, (L * 2) * NB + g + ONE)
                    sp.dma_start(xt, x_rows(g)).then_inc(x_loaded, 16)
                    sp.wait_ge(qk_kept_act, (L * NB + g) * 4 + 2 + ONE)
                    sp.wait_ge(qk_kept_dve, (L * NB + g) * 4 + 2 + ONE)
                    sp.dma_start(q_dram[bass.ds(g, 1)].rearrange("a r t h c -> (a r) (t h c)"),
                                 q_out[0:KROWS].rearrange("p t h c -> p (t h c)")).then_inc(q_stored, 16)
                sp.wait_ge(q_stored, (L + 1) * NB * 16 + ONE)
                sp.sem_inc(seen, 1)
                phase_barrier(sp, L, 0)

                with sp.Fori(0, NB) as nb:
                    sp.wait_ge(pv_done, (L * NB + nb) * (NS * B_QUADS) + ONE)
                    sp.sem_inc(seen, 1)
                    sp.wait_ge(qt_loaded, (L * NB + nb) * 16 + ONE)
                    sp.sem_inc(seen, 1)
                    sp.dma_start(q_t[0:KROWS, bass.ds(nb % 2, 1)].rearrange("p a t h c -> p (a t h c)"),
                                 q_dram[bass.ds(nb, 1)].rearrange("a r t h c -> (a r) (t h c)")).then_inc(qt_loaded, 16)
                    with sp.Fori(0, NS) as q:
                        ia = (L * NB + nb) * NS + q
                        sp.wait_ge(a_scored, ia * A_BLOCKS + (CREDIT_SCORED - A_BLOCKS))
                        sp.sem_inc(seen, 1)
                        sp.wait_ge(qa_loaded, ia * 16 + ONE)
                        sp.dma_start(q_a[:, bass.ds(q % 2, 1)].rearrange("p a h c -> p (a h c)"),
                                     q_dram[bass.ds(nb, 1), :, bass.ds(q, 1)].rearrange("a r t h c -> (a r) (t h c)")).then_inc(qa_loaded, 16)
                        for c in range(NC):
                            sp.wait_ge(mask_made, ia * NC + (c - 1 + CREDIT_MASK))
                            sp.dma_start(adj_in[:, c % 2, :],
                                         adj[bass.ds(nb * TILE + q * P, P), c * CHUNK:(c + 1) * CHUNK]).then_inc(adj_loaded[c % 2], 16)
                phase_barrier(sp, L, 1)

                sp.dma_start(wts, w_dram[bass.ds(L, 1)].rearrange("a p c -> (a p) c")).then_inc(w_here, 16)
                with sp.Fori(0, NB) as g:
                    sp.wait_ge(xn_ready, (L * 2 + 1) * NB + g + ONE)
                    sp.dma_start(xt, x_rows(g)).then_inc(x_loaded, 16)
                    sp.dma_start(o_in, o_dram[bass.ds(g, 1)].rearrange("a p b c -> (a p) b c")).then_inc(o_loaded, 16)
                    sp.wait_ge(x3_ready, L * NB + g + 1 + ONE)
                    sp.dma_start(x_rows(g), x3.rearrange("p (t c) -> p t c", t=NS)).then_inc(out_stored, 16)
                sp.wait_ge(out_stored, (L + 1) * NB * 16 + ONE)
                sp.sem_inc(seen, 1)
                phase_barrier(sp, L, 2)

        @block.tensor
        def _(pe):
            for s in from_one["pe"]:
                pe.sem_inc(s, ONE)
            pe.sem_inc(a_scored, CREDIT_SCORED)
            pe.sem_inc(mask_turned, CREDIT_MASK)
            pe.sem_inc(pv_done, CREDIT_PV)
            pe.wait_ge(set_up, 5)

            def turn_normed(gx):
                pe.wait_ge(xn_ready, gx + 1 + ONE)
                pe.wait_ge(xn_kept, gx + ONE)
                for t in range(NS):
                    mm = pe.transpose(PS[:, 0, t * P:(t + 1) * P], xn[:, t, :], idf[:])
                mm.then_inc(xn_turned, 1)

            def project(L):
                with pe.Fori(0, NB) as g:
                    gi, gx = L * NB + g, L * 2 * NB + g
                    turn_normed(gx)
                    pe.wait_ge(xn_kept, gx + 1 + ONE)
                    pe.wait_ge(v_kept, gi + ONE)
                    pe.wait_ge(parts_ready, gi + ONE)
                    for t in range(NS):
                        mm = pe.matmul(PS[:, 1 + t, 0:384], xn_t[:, t * P:(t + 1) * P], wts[:, C_QKV:C_PROJ],
                                       start=True, stop=True)
                    mm.then_inc(qkv_ready, 1)
                    pe.wait_ge(parts_ready, gi + 1 + ONE)
                    for i in range(HEADS):
                        kept = qk_kept_dve if i % 2 else qk_kept_act
                        pe.wait_ge(kept, gi * 4 + i // 2 + ONE)
                        bank = PS[:, 6 + i % 2, :].bitcast(BF16)
                        for j in range(2):
                            hk = 2 * i + j
                            for r, first in enumerate(Q_PAIRS if hk < HEADS else K_PAIRS):
                                for t in range(NS):
                                    pair = parts[:, t * 2 * HEADS + hk, first:first + 2, :].rearrange("p a d -> p (a d)")
                                    mm = pe.transpose(bank[32 * r:32 * r + 32, (j * NS + t) * P:(j * NS + t + 1) * P],
                                                      pair, idb[:])
                        mm.then_inc(qk_turned, 1)

            def ring_slot(ia, ib, use, a, b):
                (kind, n), wrapped = slot_before(use, a, b)
                if kind == "b":
                    pe.wait_ge(b_exped, ib * B_PAIRS + (n + 1 - (B_PAIRS if wrapped else 0) + CREDIT_EXPED))
                else:
                    pe.wait_ge(mask_kept, ia * NC + (n + 1 - (NC if wrapped else 0) + CREDIT_KEPT))
                return 2 * slot_of[use]

            def score_a(ia, q, mb, h):
                k = mb * HEADS + h
                pe.wait_ge(a_maxed, ia * A_BLOCKS + (k - 1 + CREDIT_MAXED))
                pe.matmul(ps_a[:, k % 2, :], q_a[:, bass.ds(q % 2, 1), h, :].rearrange("p a c -> p (a c)"),
                          k_t[0:KROWS, h, mb * TILE:(mb + 1) * TILE], start=True, stop=True).then_inc(a_scored, 1)

            def turn_mask(ia, ib, c, a, b):
                bank = ps_b[:, ring_slot(ia, ib, ("m", c), a, b), :].bitcast(BF16)
                pe.wait_ge(mask_made, ia * NC + (c + 1 + CREDIT_MASK))
                for i in range(CHUNK // P):
                    mm = pe.transpose(bank[:, i * P:(i + 1) * P], mask_n[:, c % 2, i * P:(i + 1) * P], idb[:])
                mm.then_inc(mask_turned, 1)

            def score_b(ia, ib, nb, q, s, h, a):
                use = ("b", s * 4 + h // 2)
                if h % 2 == 0:
                    ring_slot(ia, ib, use, a, True)
                bank = ps_b[:, 2 * slot_of[use] + h % 2, :]
                masked = s < B_MASKS and h in POOL_HEADS
                mm = pe.matmul(bank, k_t[0:KROWS + MROWS, h, bass.ds(q * (STEPS * P) + s * P, P)],
                               q_t[0:KROWS + MROWS, bass.ds(nb % 2, 1), :, h, :], start=True, stop=masked)
                if not masked:
                    mm = pe.matmul(bank, idb[:], mask_t[:, bass.ds((nb % 2) * MT + q * STEPS + s, 1), :].rearrange("p a c -> p (a c)"),
                                   start=False, stop=True)
                if h % 2 == 1:
                    mm.then_inc(b_scored, 1)

            def gather_v(ib, t):
                s, quad = t // 2, t % 2
                pe.wait_ge(b_exped, ib * B_PAIRS + (2 * t + 2 + CREDIT_EXPED))
                if s < B_MASKS:
                    pe.wait_ge(p_masked, ib * B_POOLED + (len(POOL_OPS) * s + 2 + quad + ONE))
                if quad == 0:
                    pe.wait_ge(v_set, ib * STEPS + (s + 1))
                for j in range(4):
                    mm = pe.matmul(ps_o[32 * j:32 * j + 32, quad, :], v_cur[:, s % 2, 4 * quad + j, :],
                                   p_buf[:, t % P_SLOTS, j, :], start=False, stop=False, skip_group_check=True)
                mm.then_inc(pv_done, 1)

            def body(ia, ib, nb, q, a, b):
                if a:
                    pe.wait_ge(qa_loaded, ia * 16 + 16 + ONE)
                for s in range(STEPS):
                    for quad in range(2):
                        if a and quad == 1 and s % 2 == 1:
                            turn_mask(ia, ib, s // 2, a, b)
                        for kind, j in ("a0", "b0", "b1", "a1", "b2", "a2", "b3", "a3"):
                            if kind == "a" and a:
                                score_a(ia, q, s, 4 * quad + int(j))
                            if kind == "b" and b:
                                score_b(ia, ib, nb, q, s, 4 * quad + int(j), a)
                        t = 2 * s + quad
                        if b and t >= LAG:
                            gather_v(ib, t - LAG)
                if b:
                    for t in range(B_QUADS - LAG, B_QUADS):
                        gather_v(ib, t)

            def turn_neg(ja):
                pe.wait_ge(neg_ready, ja + 1)
                bank = ps_a[:, 0, :].bitcast(BF16)
                for t in range(NS):
                    mm = pe.transpose(bank[KROWS:KROWS + MROWS, t * P:(t + 1) * P],
                                      neg_p[:, t, :, :].rearrange("p a h -> p (a h)"), idb[:])
                mm.then_inc(neg_turned, 1)

            def start_b(jb):
                pe.wait_ge(qt_loaded, jb * 16 + 16 + ONE)
                pe.wait_ge(neg_kept, jb * 2 + 2)
                pe.wait_ge(mask_kept, jb * NS * NC + (NS * NC + CREDIT_KEPT))
                pe.wait_ge(o_kept_act, jb + ONE)
                pe.wait_ge(o_kept_dve, jb + ONE)
                for h in range(HEADS):
                    j = h % 4
                    pe.matmul(ps_o[32 * j:32 * j + 32, h // 4, :], zeros[:], k_t[:, 0, 0:TILE],
                              start=True, stop=False, skip_group_check=True)

            def attend(L):
                with pe.Fori(0, NS) as q:
                    body(L * NB * NS + q, None, None, q, True, False)
                turn_neg(L * NB)
                with pe.Fori(0, NB - 1) as nb:
                    start_b(L * NB + nb)
                    with pe.Fori(0, NS) as q:
                        ib = (L * NB + nb) * NS + q
                        body(ib + NS, ib, nb, q, True, True)
                    turn_neg(L * NB + nb + 1)
                start_b(L * NB + (NB - 1))
                with pe.Fori(0, NS) as q:
                    body(None, (L * NB + (NB - 1)) * NS + q, NB - 1, q, False, True)

            def feed_forward(L):
                with pe.Fori(0, NB) as g:
                    gi, gx = L * NB + g, (L * 2 + 1) * NB + g
                    pe.wait_ge(o_loaded, gi * 16 + 16)
                    pe.wait_ge(attn_ready, gi + ONE)
                    for t in range(NS):
                        for half in range(2):
                            i = 2 * t + half
                            mm = pe.transpose(PS[:, i // 4, (i % 4) * P:(i % 4 + 1) * P],
                                              o_in[:, half, t * P:(t + 1) * P], idf[:])
                    mm.then_inc(o_turned, 1)
                    pe.wait_ge(attn_ready, gi + 1 + ONE)
                    for t in range(NS):
                        mm = pe.transpose(PS[:, 2, t * P:(t + 1) * P], attn[:, t * P:(t + 1) * P], idf[:])
                    mm.then_inc(attn_turned, 1)
                    pe.wait_ge(attn_kept, gi + 1)
                    pe.wait_ge(x3_ready, gi + ONE)
                    for t in range(NS):
                        mm = pe.matmul(PS[:, 3, t * P:(t + 1) * P], attn_t[:, t * P:(t + 1) * P],
                                       wts[:, C_PROJ:C_W1], start=True, stop=True)
                    mm.then_inc(proj_ready, 1)
                    turn_normed(gx)
                    pe.wait_ge(xn_kept, gx + 1 + ONE)
                    pe.wait_ge(gelu_done, gi * 4 + ONE)
                    for f in range(4):
                        pe.matmul(PS[:, 4 + f, :], wts[:, C_W1 + f * P:C_W1 + (f + 1) * P], xn_t,
                                  start=True, stop=True).then_inc(hid_ready, 1)
                    pe.wait_ge(gelu_done, gi * 4 + 4 + ONE)
                    for t in range(NS):
                        for f in range(4):
                            mm = pe.matmul(PS[:, 3, t * P:(t + 1) * P], g_t[:, f, t * P:(t + 1) * P],
                                           wts[:, C_W2 + f * P:C_W2 + (f + 1) * P], start=f == 0, stop=f == 3)
                    mm.then_inc(ff_ready, 1)

            with pe.Fori(0, LAYERS) as L:
                pe.wait_ge(w_here, L * 32 + 16)
                pe.sem_inc(seen, 1)
                project(L)
                phase_barrier(pe, L, 0)
                attend(L)
                phase_barrier(pe, L, 1)
                pe.wait_ge(w_here, L * 32 + 32)
                pe.sem_inc(seen, 1)
                feed_forward(L)
                phase_barrier(pe, L, 2)

        @block.scalar
        def _(act):
            for s in from_one["act"]:
                act.sem_inc(s, ONE)
            act.sem_inc(b_exped, CREDIT_EXPED)
            act.sem_inc(mask_kept, CREDIT_KEPT)
            act.dma_start(idb[:], ident).then_inc(w_loaded, 16)
            act.dma_start(idf[:], ident_f).then_inc(w_loaded, 16)
            act.dma_start(head_sel[KROWS:P, :], head_rows).then_inc(w_loaded, 16)
            act.wait_ge(w_loaded, 48)
            act.drain().then_inc(set_up, 1)

            def keep_normed(gx, scale_col, bias_col):
                act.wait_ge(xn_turned, gx + 1 + ONE)
                nc.scalar.activation(xn_t, PS[:, 0, :], ACT.Identity, bias=wts[:, bias_col:bias_col + 1],
                                     scale=wts[:, scale_col:scale_col + 1]).then_inc(xn_kept, 1)

            def project(L):
                with act.Fori(0, NB) as g:
                    gi, gx = L * NB + g, L * 2 * NB + g
                    act.wait_ge(qkv_ready, gi + ONE)
                    keep_normed(gx, C_G1, C_BE1)
                    act.wait_ge(qkv_ready, gi + 1 + ONE)
                    nc.scalar.activation(v_sb[:, bass.ds(g * NS, NS)].rearrange("p t h d -> p t (h d)"),
                                         PS[:, 1:5, 256:384], ACT.Copy).then_inc(v_kept, 1)
                    act.wait_ge(q_stored, gi * 16 + ONE)
                    for i in range(0, HEADS, 2):
                        act.wait_ge(qk_turned, gi * 8 + (i + 1) + ONE)
                        keep_turned(nc.scalar.copy, g, i).then_inc(qk_kept_act, 1)

            def exp_pair(ib, pair):
                t, j = pair // 2, 2 * (pair % 2)
                slot = 2 * slot_of[("b", pair)]
                act.wait_ge(b_scored, ib * B_PAIRS + (pair + 1))
                if j == 0:
                    act.wait_ge(pv_done, ib * B_QUADS + (t - P_SLOTS + 1 + CREDIT_PV))
                nc.scalar.activation(p_buf[:, t % P_SLOTS, j:j + 2, :], ps_b[:, slot:slot + 2, :],
                                     ACT.Exp, scale=SCALE).then_inc(b_exped, 1)

            def keep_mask(ia, nb, q, c):
                act.wait_ge(mask_turned, ia * NC + (c + 1 + CREDIT_MASK))
                n = CHUNK // P
                nc.scalar.activation(mask_t[:, bass.ds((nb % 2) * MT + c * n, n), bass.ds(q * P, P)],
                                     ps_b[:, 2 * slot_of[("m", c)], :].bitcast(BF16).rearrange("p (m c) -> p m c", m=n),
                                     ACT.Copy).then_inc(mask_kept, 1)

            def make_mask01(ib, nb, q, s):
                act.wait_ge(p_masked, ib * B_POOLED + (len(POOL_OPS) * max(s - 1, 0) + ONE))
                nc.scalar.activation(mask01[:, s % 2, :],
                                     mask_t[:, bass.ds((nb % 2) * MT + q * STEPS + s, 1), :].rearrange("p a c -> p (a c)"),
                                     ACT.Copy, bias=1.0, scale=-1.0 / MASKED).then_inc(mask01_made, 1)

            def set_v(ib, q, s):
                act.wait_ge(pv_done, ib * B_QUADS + (2 * s - 2 + CREDIT_PV))
                nc.scalar.activation(v_cur[:, s % 2, :, 0:HD],
                                     v_sb[:, bass.ds(q * STEPS + s, 1), :, :].rearrange("p a h d -> p (a h) d"),
                                     ACT.Copy).then_inc(v_set, 1)

            def body(ia, ib, nba, nb, q, a, b):
                if b:
                    make_mask01(ib, nb, q, 0)
                for s in range(STEPS):
                    for k in range(4):
                        if a and s % 2 == 1 and k == 2:
                            keep_mask(ia, nba, q, s // 2)
                        if b:
                            exp_pair(ib, 4 * s + k)
                            if k == 0 and s + 1 < B_MASKS:
                                make_mask01(ib, nb, q, s + 1)
                            if k == 1:
                                set_v(ib, q, s)

            def keep_neg(ja, nb):
                act.wait_ge(neg_turned, ja + 1 + ONE)
                keep_neg_half(nc.scalar.copy, nb, 0).then_inc(neg_kept, 1)

            def store_o(jb, nb):
                act.wait_ge(pv_done, jb * (NS * B_QUADS) + (NS * B_QUADS + CREDIT_PV))
                act.wait_ge(o_stored, jb * 16 + ONE)
                nc.scalar.copy(o_sb[:, 0, :], ps_o[:, 0, :]).then_inc(o_kept_act, 1)
                act.wait_ge(o_kept_act, jb + 1 + ONE)
                act.wait_ge(o_kept_dve, jb + 1 + ONE)
                act.dma_start(o_dram[bass.ds(nb, 1)].rearrange("a p b c -> (a p) (b c)"),
                              o_sb[:].rearrange("p b c -> p (b c)")).then_inc(o_stored, 16)

            def attend(L):
                with act.Fori(0, NS) as q:
                    body(L * NB * NS + q, None, 0, None, q, True, False)
                keep_neg(L * NB, 0)
                with act.Fori(0, NB - 1) as nb:
                    with act.Fori(0, NS) as q:
                        ib = (L * NB + nb) * NS + q
                        body(ib + NS, ib, nb + 1, nb, q, True, True)
                    store_o(L * NB + nb, nb)
                    keep_neg(L * NB + nb + 1, nb + 1)
                with act.Fori(0, NS) as q:
                    body(None, (L * NB + (NB - 1)) * NS + q, None, NB - 1, q, False, True)
                store_o(L * NB + (NB - 1), NB - 1)
                act.wait_ge(o_stored, (L + 1) * NB * 16 + ONE)
                act.sem_inc(seen, 1)

            def feed_forward(L):
                with act.Fori(0, NB) as g:
                    gi, gx = L * NB + g, (L * 2 + 1) * NB + g
                    act.wait_ge(attn_turned, gi + 1 + ONE)
                    act.wait_ge(proj_ready, gi + ONE)
                    nc.scalar.copy(attn_t, PS[:, 2, :]).then_inc(attn_kept, 1)
                    act.wait_ge(hid_ready, gi * 4 + ONE)
                    keep_normed(gx, C_G2, C_BE2)
                    act.wait_ge(ff_ready, gi + ONE)
                    for f in range(4):
                        act.wait_ge(hid_ready, gi * 4 + (f + 1) + ONE)
                        nc.scalar.activation(g_t[:, f, :], PS[:, 4 + f, :], ACT.Gelu_apprx_tanh,
                                             bias=wts[:, C_B1 + f:C_B1 + f + 1]).then_inc(gelu_done, 1)

            with act.Fori(0, LAYERS) as L:
                act.wait_ge(w_here, L * 32 + 16)
                project(L)
                phase_barrier(act, L, 0)
                attend(L)
                phase_barrier(act, L, 1)
                act.wait_ge(w_here, L * 32 + 32)
                feed_forward(L)
                phase_barrier(act, L, 2)

        @block.vector
        def _(dve):
            for s in from_one["dve"]:
                dve.sem_inc(s, ONE)
            dve.sem_inc(a_maxed, CREDIT_MAXED)
            dve.sem_inc(mask_made, CREDIT_MASK)

            def until(s, value):
                dve.wait_ge(s, value)
                dve.sem_inc(seen, 1)

            dve.memset(zeros[:], 0.0)
            dve.memset(minus_half[:], -0.5)
            dve.memset(v_cur[:], 0.0)
            dve.memset(rlast[:], 0.0)
            dve.drain()
            dve.memset(v_cur[:, :, :, HD:HD + 1], 1.0)
            dve.memset(k_t[KROWS:P, :, :], 1.0)
            dve.drain()
            dve.wait_ge(w_loaded, 48)
            for h in range(HEADS):
                dve.tensor_scalar(k_t[KROWS:P, h, :], k_t[KROWS:P, h, :], head_sel[KROWS:P, h:h + 1], None, ALU.mult)
            dve.drain().then_inc(set_up, 4)

            def norm(src, gx):
                for t in range(NS):
                    dve.bn_stats(stats[:, t, :], src[:, t, :])
                dve.drain()
                for t in range(NS):
                    last = dve.bn_aggr(mv[:, t, :], stats[:, t, :])
                last.then_inc(var_ready, 1)
                until(rstd_ready, gx + 1)
                until(xn_turned, gx + ONE)
                for t in range(NS):
                    last = dve.tensor_scalar(xn[:, t, :], src[:, t, :], mv[:, t, 0:1], rstd[:, t:t + 1],
                                             ALU.subtract, ALU.mult)
                last.then_inc(xn_ready, 1)

            def project(L):
                with dve.Fori(0, NB) as g:
                    gi, gx = L * NB + g, L * 2 * NB + g
                    until(x_loaded, gx * 16 + 16)
                    norm(xt, gx)
                    until(v_kept, gi + 1 + ONE)
                    until(qk_turned, gi * 8 + ONE)
                    qk = PS[:, 1:5, 0:256].rearrange("p t (g d) -> p t g d", d=HD)
                    p4 = parts.rearrange("p (t g) a d -> p t g a d", t=NS)
                    r4 = rest.rearrange("p (t g) d -> p t g d", t=NS)
                    dve.tensor_copy(p4[:, :, :, 0, :], qk)
                    dve.drain()
                    dve.tensor_tensor(r4, qk, p4[:, :, :, 0, :], ALU.subtract)
                    dve.tensor_copy(parts[:, :, 1, :], parts[:, :, 0, :])
                    dve.drain()
                    dve.tensor_copy(parts[:, :, 2, :], rest)
                    dve.drain()
                    dve.tensor_tensor(parts[:, :, 3, :], rest, parts[:, :, 2, :], ALU.subtract).then_inc(parts_ready, 1)
                    until(q_stored, gi * 16 + ONE)
                    for i in range(1, HEADS, 2):
                        until(qk_turned, gi * 8 + (i + 1) + ONE)
                        keep_turned(dve.tensor_copy, g, i).then_inc(qk_kept_dve, 1)

            def make_mask(ia, c):
                until(adj_loaded[c % 2], ia * (NC // 2 * 16) + (c // 2 + 1) * 16)
                until(mask_turned, ia * NC + (c - 1 + CREDIT_MASK))
                until(a_maxed, ia * A_BLOCKS + (2 * HEADS * (c - 1) + CREDIT_MAXED if c else 1))
                dve.tensor_scalar(mask_n[:, c % 2, :], adj_in[:, c % 2, :], 0.0, MASKED,
                                  ALU.is_equal, ALU.mult).then_inc(mask_made, 1)

            def keep_max(ia, q):
                until(a_maxed, ia * A_BLOCKS + CREDIT_MAXED)
                dve.tensor_scalar(neg[:, bass.ds(q * HEADS, HEADS)], rlast[:], -1.0, None, ALU.mult).then_inc(neg_set, 1)

            def body(ia, q, jn):
                make_mask(ia, 0)
                for mb in range(MB):
                    c = mb // 2
                    if mb % 2 == 0:
                        until(mask_made, ia * NC + (c + 1 + CREDIT_MASK))
                    for h in range(HEADS):
                        k = mb * HEADS + h
                        if mb == 0 and h == 4:
                            keep_max(ia, q)
                        if mb % 2 == 1 and h == 4 and c + 1 < NC:
                            make_mask(ia, c + 1)
                        if mb == MB - 1 and h == 0:
                            until(neg_set, jn + (1 + ONE))
                        until(a_maxed, ia * A_BLOCKS + (k + 1 - SPILLS + CREDIT_MAXED))
                        until(a_scored, ia * A_BLOCKS + (k + 1 + CREDIT_SCORED))
                        first = LOWEST if mb == 0 else rmax[:, h:h + 1]
                        into = rlast if mb == MB - 1 else rmax
                        dve.tensor_tensor_reduce(spill[:, k % SPILLS, :], ps_a[:, k % 2, :],
                                                 mask_n[:, c % 2, (mb % 2) * TILE:(mb % 2 + 1) * TILE],
                                                 1.0, first, ALU.add, ALU.max, into[:, h:h + 1]).then_inc(a_maxed, 1)

            def sub_blocks(ja, nb):
                with dve.Fori(0, NS) as q:
                    body(ja * NS + q, q, ja * (NS + 1) + q)
                keep_max((ja + 1) * NS, NS)
                until(neg_set, ja * (NS + 1) + (NS + 1 + ONE))
                split_neg(ja, nb)

            def split_neg(ja, nb):
                n3 = neg[:, HEADS:].rearrange("p (t h) -> p t h", t=NS)
                until(neg_turned, ja + ONE)
                dve.tensor_copy(neg_p[:, :, 0, :], n3)
                dve.drain()
                dve.tensor_tensor(n3, n3, neg_p[:, :, 0, :], ALU.subtract)
                dve.drain()
                dve.tensor_copy(neg_p[:, :, 1, :], n3)
                dve.drain()
                dve.tensor_tensor(neg_p[:, :, 2, :], n3, neg_p[:, :, 1, :], ALU.subtract).then_inc(neg_ready, 1)

            def keep_neg(ja, nb):
                until(neg_kept, ja * 2 + 1)
                keep_neg_half(dve.tensor_copy, nb, 1).then_inc(neg_kept, 1)

            def keep_o(jb):
                until(pv_done, jb * (NS * B_QUADS) + (NS * B_QUADS + CREDIT_PV))
                until(o_stored, jb * 16 + ONE)
                dve.tensor_copy(o_sb[:, 1, :], ps_o[:, 1, :]).then_inc(o_kept_dve, 1)

            def attend(L):
                sub_blocks(L * NB, 0)
                keep_neg(L * NB, 0)
                with dve.Fori(0, NB - 1) as nb:
                    sub_blocks(L * NB + nb + 1, nb + 1)
                    keep_o(L * NB + nb)
                    keep_neg(L * NB + nb + 1, nb + 1)
                keep_o(L * NB + (NB - 1))

            def feed_forward(L):
                with dve.Fori(0, NB) as g:
                    gi, gx = L * NB + g, (L * 2 + 1) * NB + g
                    until(o_turned, gi + 1)
                    rows = PS[:, 0:2, :].rearrange("p b (g d) -> p (b g) d", d=32)
                    sums = rsum.rearrange("p (g d) -> p g d", d=1)
                    dve.reciprocal(sums, rows[:, :, HD:HD + 1])
                    dve.drain()
                    until(attn_turned, gi + ONE)
                    dve.tensor_tensor(attn.rearrange("p (g d) -> p g d", d=HD), rows[:, :, 0:HD],
                                      sums.broadcast_to([P, NS * HEADS, HD]), ALU.mult).then_inc(attn_ready, 1)
                    until(x_loaded, gx * 16 + 16)
                    bp = wts[:, C_BP:C_B2].rearrange("p (a c) -> p a c", a=1).broadcast_to([P, NS, P])
                    b2 = wts[:, C_B2:C_G1].rearrange("p (a c) -> p a c", a=1).broadcast_to([P, NS, P])
                    x2v = x2.rearrange("p (t c) -> p t c", t=NS)
                    dve.tensor_tensor(x2v, xt, bp, ALU.add)
                    dve.drain()
                    until(proj_ready, gi + 1 + ONE)
                    dve.tensor_tensor(x2, PS[:, 3, :], x2, ALU.add)
                    dve.drain()
                    norm(x2v, gx)
                    dve.drain()
                    dve.tensor_tensor(x2v, x2v, b2, ALU.add)
                    dve.drain()
                    until(ff_ready, gi + 1 + ONE)
                    until(out_stored, gi * 16 + ONE)
                    dve.tensor_tensor(x3, PS[:, 3, :], x2, ALU.add).then_inc(x3_ready, 1)

            with dve.Fori(0, LAYERS) as L:
                until(w_here, L * 32 + 16)
                project(L)
                phase_barrier(dve, L, 0)
                attend(L)
                phase_barrier(dve, L, 1)
                until(w_here, L * 32 + 32)
                feed_forward(L)
                phase_barrier(dve, L, 2)

        @block.gpsimd
        def _(pool):
            for s in from_one["pool"]:
                pool.sem_inc(s, ONE)
            pool.wait_ge(set_up, 5)

            def rstds(gx0):
                with pool.Fori(0, NB) as g:
                    pool.wait_ge(var_ready, gx0 + g + 1)
                    pool.sem_inc(seen, 1)
                    pool.tensor_scalar(ve, mv[:, :, 1], EPS, None, ALU.add)
                    pool.drain()
                    pool.tensor_tensor(rstd, ve, minus_half[:], ALU.pow).then_inc(rstd_ready, 1)

            def masks(L):
                with pool.Fori(0, NB) as nb:
                    with pool.Fori(0, NS) as q:
                        ib = (L * NB + nb) * NS + q
                        for s in range(B_MASKS):
                            for i, (h, n) in enumerate(POOL_OPS):
                                t, j = 2 * s + h // 4, h % 4
                                if i == 0:
                                    pool.wait_ge(mask01_made, ib * B_MASKS + (s + 1))
                                    pool.sem_inc(seen, 1)
                                pool.wait_ge(b_exped, ib * B_PAIRS + (4 * s + h // 2 + 1 + CREDIT_EXPED))
                                p = p_buf[:, t % P_SLOTS, j:j + n, :].bitcast(I32)
                                pool.tensor_tensor(p, p, mask01[:, s % 2, :].rearrange("p (a c) -> p a c", a=1).broadcast_to([P, n, TILE]),
                                                   ALU.mult).then_inc(p_masked, 1)

            with pool.Fori(0, LAYERS) as L:
                rstds(L * 2 * NB)
                phase_barrier(pool, L, 0)
                masks(L)
                phase_barrier(pool, L, 1)
                rstds((L * 2 + 1) * NB)
                phase_barrier(pool, L, 2)


def kernel(**inputs):
    import numpy as np
    import ml_dtypes
    import concourse.bacc as bacc
    from concourse.bass_utils import run_bass_kernel_spmd

    nc = bacc.Bacc("TRN2", target_bir_lowering=False, num_devices=1, dynamic_dma_scratch_size=1024)
    arrays, aps = {}, {}

    def give(name, a):
        a = np.ascontiguousarray(a)
        arrays[f"in_{name}"] = a
        aps[name] = nc.dram_tensor(f"in_{name}", a.shape, mybir.dt.from_np(a.dtype), kind="ExternalInput").ap()
        return aps[name]

    give("x", inputs["x"])
    give("adj", inputs["adj"])
    weights = [{n: give(f"L{l}_gnn_{n}", inputs[f"L{l}_gnn_{n}"]) for n in NAMES} for l in range(LAYERS)]
    ident = give("ident", np.eye(P, dtype=ml_dtypes.bfloat16))
    ident_f = give("ident_f", np.eye(P, dtype=np.float32))
    rows = np.zeros((P - KROWS, HEADS), np.float32)
    for i in range(MROWS):
        rows[i, i % HEADS] = 1.0
    head_rows = give("head_rows", rows)
    out = nc.dram_tensor("out_dram", (N, P), F32, kind="ExternalOutput").ap()
    gnn_kernel(nc, aps["x"], aps["adj"], weights, ident, ident_f, head_rows, out)
    r = run_bass_kernel_spmd(nc, [arrays], core_ids=[0])
    return r.results[0]["out_dram"]
```

```python
from contextlib import ExitStack

import concourse.bass as bass
from concourse import mybir

ALU = mybir.AluOpType
ACT = mybir.ActivationFunctionType
F32 = mybir.dt.float32
BF16 = mybir.dt.bfloat16
I32 = mybir.dt.int32

P = 128
N = 4096
HEADS, HD = 8, 16
FF = 512
LAYERS = 2
EPS = 1e-5
SCALE = HD ** -0.5

TILE = 512
NB = N // TILE
NS = TILE // P
MT = N // P
MB = N // TILE
STEPS = MT // NS
CHUNK = 1024
NC = N // CHUNK
PARTS = 3
KROWS = 2 * PARTS * HD
MROWS = PARTS * HEADS
MASKED = -(2.0 ** 100)
LOWEST = -3e38
SPILLS = 2
P_SLOTS = 4
LAG = 2
POOL_OPS = ((0, 2), (2, 1), (4, 2))
POOL_OPS_LAST = ((0, 1), (2, 1), (4, 1))

Q_HIGH, Q_MIDDLE, Q_LOW = slice(0, 2), 3, 4
K_HIGH, K_MIDDLE, K_LOW = slice(3, 5), 1, 0
HIGH, MIDDLE = 2, 5

C_QKV, C_PROJ, C_W1, C_W2 = 0, 384, 512, 1024
C_BP, C_B2, C_G1 = 1536, 1664, 1792
C_BE1, C_G2, C_BE2, C_B1 = 1793, 1794, 1795, 1796
WCOLS = 1800

NAMES = ("w_qkv", "w_proj", "b_proj", "w1", "b1", "w2", "b2", "g1", "be1", "g2", "be2")


def gnn_kernel(nc, x, adj, weights, ident, ident_f, head_rows, out):
    ctx = ExitStack()
    with ctx:
        def sb(name, shape, dt):
            return ctx.enter_context(nc.sbuf_tensor(name, shape, dt))

        def sem(name):
            return ctx.enter_context(nc.semaphore(name))

        q_dram = nc.dram_tensor("q_parts_dram", (NB, KROWS, NS, HEADS, P), BF16, kind="Internal").ap()
        o_dram = nc.dram_tensor("attn_dram", (NB, P, 2, TILE), F32, kind="Internal").ap()
        w_dram = nc.dram_tensor("weights_dram", (LAYERS, P, WCOLS), F32, kind="Internal").ap()

        idb = sb("idb", [P, P], BF16)
        idf = sb("idf", [P, P], F32)
        zeros = sb("zeros", [P, 32], BF16)
        minus_half = sb("minus_half", [P, NS], F32)
        k_t = sb("k_t", [P, HEADS, N], BF16)
        v_sb = sb("v_sb", [P, MT, HEADS, HD], F32)
        q_t = sb("q_t", [P, 2, NS, HEADS, P], BF16)
        q_a = sb("q_a", [KROWS, 2, HEADS, P], BF16)
        adj_in = sb("adj_in", [P, 2, CHUNK], I32)
        mask_n = sb("mask_n", [P, 2, CHUNK], BF16)
        arena = sb("arena", [P, 2 * MT, TILE], BF16)
        mask_t = arena
        p_buf = sb("p_buf", [P, P_SLOTS, 4, TILE], F32)
        mask01 = sb("mask01", [P, 2, TILE], I32)
        spill = sb("spill", [P, SPILLS, TILE], BF16)
        v_cur = sb("v_cur", [P, 2, HEADS, 32], F32)
        rmax = sb("rmax", [P, HEADS], F32)
        rlast = sb("rlast", [P, HEADS], F32)
        neg = sb("neg", [P, (NS + 1) * HEADS], F32)
        neg_p = sb("neg_p", [P, NS, PARTS, HEADS], BF16)

        flat = arena[:].rearrange("p a b -> p (a b)")
        at = [0]

        def carve(cols, dt):
            width = 2 if dt == F32 else 1
            a = flat[:, at[0]:at[0] + cols * width]
            at[0] += cols * width
            return a.bitcast(F32) if dt == F32 else a

        wts = carve(WCOLS, F32)
        xt = carve(NS * P, F32).rearrange("p (t c) -> p t c", t=NS)
        xn = carve(NS * P, F32).rearrange("p (t c) -> p t c", t=NS)
        xn_t = carve(TILE, F32)
        stats = carve(NS * 6, F32).rearrange("p (t c) -> p t c", t=NS)
        mv = carve(NS * 2, F32).rearrange("p (t c) -> p t c", t=NS)
        ve = carve(NS, F32)
        rstd = carve(NS, F32)
        part_cols = NS * 2 * HEADS * KROWS
        p_flat = p_buf[:].rearrange("p a b c -> p (a b c)").bitcast(BF16)
        parts = [p_flat[:, i * part_cols:(i + 1) * part_cols].rearrange("p (g a d) -> p g a d", a=2 * PARTS, d=HD)
                 for i in range(2)]
        qk_parts = [(p[:, 0:NS * HEADS], p[:, NS * HEADS:]) for p in parts]
        rest = carve(NS * 2 * HEADS * HD, F32).rearrange("p (g d) -> p g d", d=HD)
        q_rest, k_rest = rest[:, 0:NS * HEADS], rest[:, NS * HEADS:]
        q_out = carve(NS * HEADS * P, BF16).rearrange("p (t h c) -> p t h c", t=NS, h=HEADS)
        o_in = carve(2 * TILE, F32).rearrange("p (a c) -> p a c", a=2)
        rsum = carve(NS * HEADS, F32)
        attn = carve(NS * P, F32)
        attn_t = carve(TILE, F32)
        x2 = carve(NS * P, F32)
        x2_b = carve(NS * P, F32)
        x3 = carve(NS * P, F32)
        g_t = carve(4 * TILE, F32).rearrange("p (f c) -> p f c", f=4)
        o_sb = sb("o_sb", [P, 2, TILE], F32)

        PS = ctx.enter_context(nc.psum_tensor("PS", [P, 8, TILE], F32))
        ps_b, ps_o, ps_a = PS[:, 0:4, :], PS[:, 4:6, :], PS[:, 6:8, :]

        w_loaded, w_packed, w_here = sem("w_loaded"), sem("w_packed"), sem("w_here")
        x_copied, rows_loaded = sem("x_copied"), sem("rows_loaded")
        set_up = sem("set_up")
        phase_end = sem("phase_end")
        seen = sem("seen")
        x_loaded, var_ready, rstd_ready = sem("x_loaded"), sem("var_ready"), sem("rstd_ready")
        xn_ready, xn_turned, xn_kept = sem("xn_ready"), sem("xn_turned"), sem("xn_kept")
        qkv_ready, v_kept, qk_taken = sem("qkv_ready"), sem("v_kept"), sem("qk_taken")
        high_spread, parts_ready = sem("high_spread"), sem("parts_ready")
        qk_turned, qk_kept_act, qk_kept_dve, q_stored = (
            sem("qk_turned"), sem("qk_kept_act"), sem("qk_kept_dve"), sem("q_stored"))
        qt_loaded, qa_loaded = sem("qt_loaded"), sem("qa_loaded")
        adj_loaded = [sem("adj_loaded_0"), sem("adj_loaded_1")]
        mask_made, mask_turned, mask_kept = sem("mask_made"), sem("mask_turned"), sem("mask_kept")
        a_scored, a_maxed = sem("a_scored"), sem("a_maxed")
        neg_set = sem("neg_set")
        neg_ready, neg_turned, neg_kept_act, neg_kept_dve = (
            sem("neg_ready"), sem("neg_turned"), sem("neg_kept_act"), sem("neg_kept_dve"))
        b_scored, b_exped, pv_done, v_set = sem("b_scored"), sem("b_exped"), sem("pv_done"), sem("v_set")
        mask01_made, p_masked = sem("mask01_made"), sem("p_masked")
        o_kept_act, o_kept_dve, o_stored = sem("o_kept_act"), sem("o_kept_dve"), sem("o_stored")
        o_loaded, o_turned, attn_ready = sem("o_loaded"), sem("o_turned"), sem("attn_ready")
        attn_turned, attn_kept, proj_ready = sem("attn_turned"), sem("attn_kept"), sem("proj_ready")
        hid_ready, gelu_done, ff_ready, x3_ready, out_stored = (
            sem("hid_ready"), sem("gelu_done"), sem("ff_ready"), sem("x3_ready"), sem("out_stored"))

        A_BLOCKS = MB * HEADS
        B_PAIRS = STEPS * 4
        B_QUADS = STEPS * 2
        CREDIT_SCORED, CREDIT_MAXED = 2 * A_BLOCKS, 5
        CREDIT_MASK = 2
        CREDIT_EXPED, CREDIT_PV, CREDIT_KEPT = 2, NS * B_QUADS + 1, 2
        B_MASKS = STEPS - 1
        B_POOLED = B_MASKS * len(POOL_OPS)
        ONE = 1
        from_one = {
            "sp": (q_stored, qt_loaded, qa_loaded, out_stored),
            "pool": (p_masked,),
            "pe": (o_turned, qkv_ready, qk_turned, xn_turned, neg_turned, proj_ready, hid_ready, ff_ready, attn_turned),
            "act": (attn_kept, neg_kept_act, xn_kept, v_kept, qk_kept_act, o_kept_act, o_stored, gelu_done),
            "dve": (qk_taken, neg_kept_dve, neg_set, xn_ready, parts_ready, qk_kept_dve, o_kept_dve, attn_ready, x3_ready),
        }

        def phase_barrier(eng, L, n):
            eng.drain().then_inc(phase_end, 1)
            eng.wait_ge(phase_end, (L * 3 + (n + 1)) * 5)
            eng.sem_inc(seen, 1)

        ring = []
        for step in range(STEPS):
            ring += [("b", 4 * step), ("b", 4 * step + 1)]
            if step % 2 == 1:
                ring.append(("m", step // 2))
            ring += [("b", 4 * step + 2), ("b", 4 * step + 3)]
        assert len(ring) % 2 == 0
        slot_of = {use: i % 2 for i, use in enumerate(ring)}

        def slot_before(use, a, b):
            there = [u for u in ring if slot_of[u] == slot_of[use] and (b if u[0] == "b" else a)]
            i = there.index(use)
            return there[i - 1], i == 0

        def a_bank(k, alone):
            return (PS[:, 4 + k % 4, :], 4) if alone else (ps_a[:, k % 2, :], 2)

        def keep_turned(copy, g, i):
            bank = PS[0:KROWS, 6 + i % 2, :].bitcast(BF16)
            if i < 4:
                return copy(q_out[0:KROWS, :, 2 * i:2 * i + 2, :].rearrange("p t h c -> p h t c"),
                            bank.rearrange("p (h t c) -> p h t c", h=2, t=NS))
            return copy(k_t[0:KROWS, 2 * i - 8:2 * i - 6, bass.ds(g * TILE, TILE)],
                        bank.rearrange("p (h c) -> p h c", h=2))

        def keep_neg(copy, nb, i):
            src = ps_a[KROWS:KROWS + MROWS, min(i, 1), 0:TILE // 2].bitcast(BF16).rearrange("p (t a c) -> p t a c", t=NS, a=1)
            dst = q_t[KROWS:KROWS + MROWS, bass.ds(nb % 2, 1), :, 2 * i:2 * i + 2, :].rearrange("p a t h c -> p (a t) h c")
            return copy(dst, src.broadcast_to([MROWS, NS, 2, P]))

        block = ctx.enter_context(nc.Block())

        @block.sync
        def _(sp):
            for s in from_one["sp"]:
                sp.sem_inc(s, ONE)
            for l in range(LAYERS):
                w = weights[l]
                wd = w_dram[l]
                col = lambda a: a.rearrange("(p a) -> p a", a=1)
                row = lambda a: a.rearrange("(a p) -> a p", a=1).broadcast_to([P, P])
                sp.dma_start(wd[:, C_QKV:C_PROJ], w["w_qkv"]).then_inc(w_packed, 16)
                sp.dma_start(wd[:, C_PROJ:C_W1], w["w_proj"]).then_inc(w_packed, 16)
                sp.dma_start(wd[:, C_W1:C_W2], w["w1"]).then_inc(w_packed, 16)
                sp.dma_start(wd[:, C_W2:C_BP].rearrange("p (f c) -> p f c", f=4),
                             w["w2"].rearrange("(f p) c -> p f c", p=P)).then_inc(w_packed, 16)
                sp.dma_start(wd[:, C_BP:C_B2], row(w["b_proj"])).then_inc(w_packed, 16)
                sp.dma_start(wd[:, C_B2:C_G1], row(w["b2"])).then_inc(w_packed, 16)
                sp.dma_start(wd[:, C_G1:C_G1 + 1], col(w["g1"]), allow_slow_non_contiguous=True).then_inc(w_packed, 16)
                sp.dma_start(wd[:, C_BE1:C_BE1 + 1], col(w["be1"]), allow_slow_non_contiguous=True).then_inc(w_packed, 16)
                sp.dma_start(wd[:, C_G2:C_G2 + 1], col(w["g2"]), allow_slow_non_contiguous=True).then_inc(w_packed, 16)
                sp.dma_start(wd[:, C_BE2:C_BE2 + 1], col(w["be2"]), allow_slow_non_contiguous=True).then_inc(w_packed, 16)
                sp.dma_start(wd[:, C_B1:C_B1 + 4], w["b1"].rearrange("(f p) -> p f", p=P),
                             allow_slow_non_contiguous=True).then_inc(w_packed, 16)
            sp.dma_start(out.rearrange("(a b) c -> a (b c)", a=P), x.rearrange("(a b) c -> a (b c)", a=P)).then_inc(x_copied, 16)
            sp.wait_ge(w_packed, 16 * 11 * LAYERS)
            sp.wait_ge(x_copied, 16)

            def x_rows(g):
                return out[bass.ds(g * TILE, TILE), :].rearrange("(t p) c -> p t c", p=P)

            def load_adj(i, c):
                sp.dma_start(adj_in[:, c % 2, :], adj[bass.ds(i * P, P), c * CHUNK:(c + 1) * CHUNK]).then_inc(adj_loaded[c % 2], 16)

            load_adj(0, 0)
            with sp.Fori(0, LAYERS) as L:
                sp.dma_start(wts, w_dram[bass.ds(L, 1)].rearrange("a p c -> (a p) c")).then_inc(w_here, 16)
                def load_x(g):
                    sp.wait_ge(xn_ready, (L * 2) * NB + g + ONE)
                    sp.dma_start(xt, x_rows(g)).then_inc(x_loaded, 16)

                def store_q(g):
                    sp.wait_ge(qk_kept_act, (L * NB + g) * 4 + 2 + ONE)
                    sp.wait_ge(qk_kept_dve, (L * NB + g) * 4 + 2 + ONE)
                    sp.dma_start(q_dram[bass.ds(g, 1)].rearrange("a r t h c -> (a r) (t h c)"),
                                 q_out[0:KROWS].rearrange("p t h c -> p (t h c)")).then_inc(q_stored, 16)

                with sp.Fori(0, 2) as g:
                    load_x(g)
                with sp.Fori(0, NB - 2) as g:
                    load_x(g + 2)
                    store_q(g)
                with sp.Fori(NB - 2, NB) as g:
                    store_q(g)
                sp.wait_ge(q_stored, (L + 1) * NB * 16 + ONE)
                sp.sem_inc(seen, 1)
                phase_barrier(sp, L, 0)

                def load_sub_block(nb, q):
                    ia = (L * NB + nb) * NS + q
                    sp.wait_ge(a_scored, ia * A_BLOCKS + (CREDIT_SCORED - A_BLOCKS))
                    sp.sem_inc(seen, 1)
                    sp.wait_ge(qa_loaded, ia * 16 + ONE)
                    sp.dma_start(q_a[:, bass.ds(q % 2, 1)].rearrange("p a h c -> p (a h c)"),
                                 q_dram[bass.ds(nb, 1), :, bass.ds(q, 1)].rearrange("a r t h c -> (a r) (t h c)")).then_inc(qa_loaded, 16)
                    for c in range(1, NC):
                        sp.wait_ge(mask_made, ia * NC + (c - 1 + CREDIT_MASK))
                        load_adj(nb * NS + q, c)
                    sp.wait_ge(mask_made, ia * NC + (NC - 1 + CREDIT_MASK))
                    load_adj((nb * NS + q + 1) % (NB * NS), 0)

                with sp.Fori(0, NB) as nb:
                    with sp.Fori(0, 1) as q:
                        load_sub_block(nb, q)
                    sp.wait_ge(pv_done, (L * NB + nb) * (NS * B_QUADS) + ONE)
                    sp.sem_inc(seen, 1)
                    sp.wait_ge(qt_loaded, (L * NB + nb) * 16 + ONE)
                    sp.sem_inc(seen, 1)
                    sp.dma_start(q_t[0:KROWS, bass.ds(nb % 2, 1)].rearrange("p a t h c -> p (a t h c)"),
                                 q_dram[bass.ds(nb, 1)].rearrange("a r t h c -> (a r) (t h c)")).then_inc(qt_loaded, 16)
                    with sp.Fori(1, NS) as q:
                        load_sub_block(nb, q)
                phase_barrier(sp, L, 1)

                sp.dma_start(wts, w_dram[bass.ds(L, 1)].rearrange("a p c -> (a p) c")).then_inc(w_here, 16)
                def load_group(g):
                    sp.wait_ge(o_turned, L * NB + g + ONE)
                    sp.dma_start(o_in, o_dram[bass.ds(g, 1)].rearrange("a p b c -> (a p) b c")).then_inc(o_loaded, 16)
                    sp.wait_ge(xn_ready, (L * 2 + 1) * NB + g + ONE)
                    sp.dma_start(xt, x_rows(g)).then_inc(x_loaded, 16)

                def store_group(g):
                    sp.wait_ge(x3_ready, L * NB + g + 1 + ONE)
                    sp.dma_start(x_rows(g), x3.rearrange("p (t c) -> p t c", t=NS)).then_inc(out_stored, 16)

                with sp.Fori(0, 2) as g:
                    load_group(g)
                with sp.Fori(0, NB - 2) as g:
                    load_group(g + 2)
                    store_group(g)
                with sp.Fori(NB - 2, NB) as g:
                    store_group(g)
                sp.wait_ge(out_stored, (L + 1) * NB * 16 + ONE)
                sp.sem_inc(seen, 1)
                phase_barrier(sp, L, 2)

        @block.tensor
        def _(pe):
            for s in from_one["pe"]:
                pe.sem_inc(s, ONE)
            pe.sem_inc(a_scored, CREDIT_SCORED)
            pe.sem_inc(mask_turned, CREDIT_MASK)
            pe.sem_inc(pv_done, CREDIT_PV)
            pe.wait_ge(set_up, 5)

            def turn_normed(gx):
                pe.wait_ge(xn_ready, gx + 1 + ONE)
                pe.wait_ge(xn_kept, gx + ONE)
                for t in range(NS):
                    mm = pe.transpose(PS[:, 0, t * P:(t + 1) * P], xn[:, t, :], idf[:])
                mm.then_inc(xn_turned, 1)

            def project_group(gi, gx):
                pe.wait_ge(xn_kept, gx + 1 + ONE)
                pe.wait_ge(v_kept, gi + ONE)
                pe.wait_ge(qk_taken, gi + ONE)
                for t in range(NS):
                    mm = pe.matmul(PS[:, 1 + t, 0:384], xn_t[:, t * P:(t + 1) * P], wts[:, C_QKV:C_PROJ],
                                   start=True, stop=True)
                mm.then_inc(qkv_ready, 1)

            def turn_parts(gi, slot, batches):
                for i in batches:
                    if i == 0:
                        pe.wait_ge(high_spread, gi * 2 + 2)
                        pe.wait_ge(parts_ready, gi + 1 + ONE)
                    kept = qk_kept_dve if i % 2 else qk_kept_act
                    pe.wait_ge(kept, gi * 4 + i // 2 + ONE)
                    bank = PS[:, 6 + i % 2, :].bitcast(BF16)
                    part = qk_parts[slot][i // 4]
                    for j in range(2):
                        for t in range(NS):
                            mm = pe.transpose(bank[0:KROWS, (j * NS + t) * P:(j * NS + t + 1) * P],
                                              part[:, t * HEADS + 2 * (i % 4) + j].rearrange("p a d -> p (a d)"), idb[:])
                    mm.then_inc(qk_turned, 1)

            def project(L):
                def group(g, slot, normed):
                    gi, gx = L * NB + g, L * 2 * NB + g
                    turn_parts(gi, slot, range(0, 2))
                    project_group(gi + 1, gx + 1)
                    turn_parts(gi, slot, range(2, 8))
                    if normed:
                        turn_normed(gx + 2)

                turn_normed(L * 2 * NB)
                project_group(L * NB, L * 2 * NB)
                turn_normed(L * 2 * NB + 1)
                with pe.Fori(0, (NB - 2) // 2) as pair:
                    for slot in range(2):
                        group(pair * 2 + slot, slot, True)
                group(NB - 2, 0, False)
                turn_parts(L * NB + (NB - 1), 1, range(0, 8))

            def ring_slot(ia, ib, use, a, b):
                (kind, n), wrapped = slot_before(use, a, b)
                if kind == "b":
                    pe.wait_ge(b_exped, ib * B_PAIRS + (n + 1 - (B_PAIRS if wrapped else 0) + CREDIT_EXPED))
                else:
                    pe.wait_ge(mask_kept, ia * NC + (n + 1 - (NC if wrapped else 0) + CREDIT_KEPT))
                return 2 * slot_of[use]

            def score_a(ia, jb, nb, q, mb, h):
                k = mb * HEADS + h
                bank, banks = a_bank(k, nb is None)
                pe.wait_ge(a_maxed, ia * A_BLOCKS + (k + 1 - banks + CREDIT_MAXED))
                if k == 0 and nb is not None:
                    pe.wait_ge(neg_kept_act, jb + (1 + ONE))
                if k == 1 and nb is not None:
                    pe.wait_ge(neg_kept_dve, jb * 3 + (3 + ONE))
                pe.matmul(bank, q_a[:, bass.ds(q % 2, 1), h, :].rearrange("p a c -> p (a c)"),
                          k_t[0:KROWS, h, mb * TILE:(mb + 1) * TILE], start=True, stop=True).then_inc(a_scored, 1)

            def turn_mask(ia, ib, c, a, b):
                bank = ps_b[:, ring_slot(ia, ib, ("m", c), a, b), :].bitcast(BF16)
                pe.wait_ge(mask_made, ia * NC + (c + 1 + CREDIT_MASK))
                for i in range(CHUNK // P):
                    mm = pe.transpose(bank[:, i * P:(i + 1) * P], mask_n[:, c % 2, i * P:(i + 1) * P], idb[:])
                mm.then_inc(mask_turned, 1)

            def score_b(ia, ib, jb, nb, q, s, h, a):
                use = ("b", s * 4 + h // 2)
                if h % 2 == 0:
                    ring_slot(ia, ib, use, a, True)
                    if s == 0:
                        if h == 0:
                            pe.wait_ge(neg_kept_act, jb + (1 + ONE))
                        else:
                            pe.wait_ge(neg_kept_dve, jb * 3 + (h // 2 + ONE))
                bank = ps_b[:, 2 * slot_of[use] + h % 2, :]
                masked = s < B_MASKS and any(first <= h < first + n for first, n in (POOL_OPS if a else POOL_OPS_LAST))
                mm = pe.matmul(bank, k_t[0:KROWS + MROWS, h, bass.ds(q * (STEPS * P) + s * P, P)],
                               q_t[0:KROWS + MROWS, bass.ds(nb % 2, 1), :, h, :], start=True, stop=masked)
                if not masked:
                    mm = pe.matmul(bank, idb[:], mask_t[:, bass.ds((nb % 2) * MT + q * STEPS + s, 1), :].rearrange("p a c -> p (a c)"),
                                   start=False, stop=True)
                if h % 2 == 1:
                    mm.then_inc(b_scored, 1)

            def gather_v(ib, t):
                s, quad = t // 2, t % 2
                pe.wait_ge(b_exped, ib * B_PAIRS + (2 * t + 2 + CREDIT_EXPED))
                if s < B_MASKS:
                    pe.wait_ge(p_masked, ib * B_POOLED + (len(POOL_OPS) * s + 2 + quad + ONE))
                if quad == 0:
                    pe.wait_ge(v_set, ib * STEPS + (s + 1))
                for j in range(4):
                    mm = pe.matmul(ps_o[32 * j:32 * j + 32, quad, :], v_cur[:, s % 2, 4 * quad + j, :],
                                   p_buf[:, t % P_SLOTS, j, :], start=False, stop=False, skip_group_check=True)
                mm.then_inc(pv_done, 1)

            def body(ia, ib, jb, nb, q, a, b):
                if a:
                    pe.wait_ge(qa_loaded, ia * 16 + 16 + ONE)
                for s in range(STEPS):
                    for quad in range(2):
                        if a and quad == 1 and s % 2 == 1:
                            turn_mask(ia, ib, s // 2, a, b)
                        t = 2 * s + quad
                        order = ["a0", "b0", "b1", "a1", "b2", "a2", "b3", "a3", "g0"]
                        if t == B_QUADS - 1:
                            order = ["a0", "b0", "b1", "a1", "b2", "a2", "b3", "g0", "g1", "a3", "g2"]
                        for kind, j in order:
                            if kind == "a" and a:
                                score_a(ia, jb, nb, q, s, 4 * quad + int(j))
                            if kind == "b" and b:
                                score_b(ia, ib, jb, nb, q, s, 4 * quad + int(j), a)
                            if kind == "g" and b and t >= LAG:
                                gather_v(ib, t - LAG + int(j))

            def turn_neg(ja):
                pe.wait_ge(neg_ready, ja + 1)
                for i in range(2):
                    bank = ps_a[:, i, :].bitcast(BF16)
                    for t in range(NS):
                        mm = pe.transpose(bank[KROWS:KROWS + MROWS, t * P:(t + 1) * P],
                                          neg_p[:, t, :, :].rearrange("p a h -> p (a h)"), idb[:])
                mm.then_inc(neg_turned, 1)

            def start_b(jb):
                pe.wait_ge(qt_loaded, jb * 16 + 16 + ONE)
                pe.wait_ge(mask_kept, jb * NS * NC + (NS * NC + CREDIT_KEPT))
                pe.wait_ge(o_kept_act, jb + ONE)
                pe.wait_ge(o_kept_dve, jb + ONE)
                for h in range(HEADS):
                    j = h % 4
                    pe.matmul(ps_o[32 * j:32 * j + 32, h // 4, :], zeros[:], k_t[:, 0, 0:TILE],
                              start=True, stop=False, skip_group_check=True)

            def attend(L):
                with pe.Fori(0, NS) as q:
                    body(L * NB * NS + q, None, None, None, q, True, False)
                turn_neg(L * NB)
                with pe.Fori(0, NB - 1) as nb:
                    start_b(L * NB + nb)
                    with pe.Fori(0, NS) as q:
                        ib = (L * NB + nb) * NS + q
                        body(ib + NS, ib, L * NB + nb, nb, q, True, True)
                    turn_neg(L * NB + nb + 1)
                start_b(L * NB + (NB - 1))
                with pe.Fori(0, NS) as q:
                    body(None, (L * NB + (NB - 1)) * NS + q, L * NB + (NB - 1), NB - 1, q, False, True)

            def turn_o(gi, gx):
                pe.wait_ge(o_loaded, gi * 16 + 16)
                pe.wait_ge(attn_kept, gi + ONE)
                pe.wait_ge(xn_ready, gx + ONE)
                for t in range(NS):
                    for half in range(2):
                        i = 2 * t + half
                        mm = pe.transpose(PS[:, 1 + i // 4, (i % 4) * P:(i % 4 + 1) * P],
                                          o_in[:, half, t * P:(t + 1) * P], idf[:])
                mm.then_inc(o_turned, 1)

            def turn_attn(gi):
                pe.wait_ge(attn_ready, gi + 1 + ONE)
                for t in range(NS):
                    mm = pe.transpose(PS[:, 1, t * P:(t + 1) * P], attn[:, t * P:(t + 1) * P], idf[:])
                mm.then_inc(attn_turned, 1)

            def project_attn(gi):
                pe.wait_ge(attn_kept, gi + 1 + ONE)
                for t in range(NS):
                    mm = pe.matmul(PS[:, 2, t * P:(t + 1) * P], attn_t[:, t * P:(t + 1) * P],
                                   wts[:, C_PROJ:C_W1], start=True, stop=True)
                mm.then_inc(proj_ready, 1)

            def hidden(gi, gx, f):
                if f == 0:
                    pe.wait_ge(xn_kept, gx + 1 + ONE)
                pe.wait_ge(gelu_done, gi * 4 + f + ONE)
                pe.matmul(PS[:, 4 + f, :], wts[:, C_W1 + f * P:C_W1 + (f + 1) * P], xn_t,
                          start=True, stop=True).then_inc(hid_ready, 1)

            def second_layer(gi):
                pe.wait_ge(gelu_done, gi * 4 + 4 + ONE)
                pe.wait_ge(x3_ready, gi + ONE)
                for t in range(NS):
                    for f in range(4):
                        mm = pe.matmul(PS[:, 3, t * P:(t + 1) * P], g_t[:, f, t * P:(t + 1) * P],
                                       wts[:, C_W2 + f * P:C_W2 + (f + 1) * P], start=f == 0, stop=f == 3)
                mm.then_inc(ff_ready, 1)

            def feed_forward(L):
                gi, gx = L * NB, (L * 2 + 1) * NB
                turn_o(gi, gx)
                turn_attn(gi)
                project_attn(gi)
                with pe.Fori(0, NB - 1) as g:
                    gi, gx = L * NB + g, (L * 2 + 1) * NB + g
                    turn_normed(gx)
                    turn_o(gi + 1, gx + 1)
                    for f in range(3):
                        hidden(gi, gx, f)
                    turn_attn(gi + 1)
                    hidden(gi, gx, 3)
                    project_attn(gi + 1)
                    second_layer(gi)
                gi, gx = L * NB + (NB - 1), (L * 2 + 1) * NB + (NB - 1)
                turn_normed(gx)
                for f in range(4):
                    hidden(gi, gx, f)
                second_layer(gi)

            with pe.Fori(0, LAYERS) as L:
                pe.wait_ge(w_here, L * 32 + 16)
                pe.sem_inc(seen, 1)
                project(L)
                pe.wait_ge(rows_loaded, HEADS * 16)
                phase_barrier(pe, L, 0)
                attend(L)
                phase_barrier(pe, L, 1)
                pe.wait_ge(w_here, L * 32 + 32)
                pe.sem_inc(seen, 1)
                feed_forward(L)
                phase_barrier(pe, L, 2)

        @block.scalar
        def _(act):
            for s in from_one["act"]:
                act.sem_inc(s, ONE)
            act.sem_inc(b_exped, CREDIT_EXPED)
            act.sem_inc(mask_kept, CREDIT_KEPT)
            act.dma_start(idb[:], ident).then_inc(w_loaded, 16)
            act.dma_start(idf[:], ident_f).then_inc(w_loaded, 16)
            act.wait_ge(w_loaded, 32)
            act.drain().then_inc(set_up, 1)
            for h in range(HEADS):
                act.dma_start(k_t[KROWS:P, h, :].rearrange("p (a c) -> p a c", c=TILE),
                              head_rows[:, h:h + 1, :].broadcast_to([P - KROWS, MB, TILE])).then_inc(rows_loaded, 16)

            def keep_normed(gx, scale_col, bias_col):
                act.wait_ge(xn_turned, gx + 1 + ONE)
                nc.scalar.activation(xn_t, PS[:, 0, :], ACT.Identity, bias=wts[:, bias_col:bias_col + 1],
                                     scale=wts[:, scale_col:scale_col + 1]).then_inc(xn_kept, 1)

            def keep_projected(gi, g, slot):
                act.wait_ge(qkv_ready, gi + 1 + ONE)
                if slot is not None:
                    act.wait_ge(qk_turned, (gi - 1) * 8 + ONE)
                for part, first in zip(qk_parts[slot or 0], (0, P)):
                    nc.scalar.activation(part[:, :, HIGH, :].rearrange("p (t h) d -> p t h d", t=NS),
                                         PS[:, 1:5, first:first + P].rearrange("p t (h d) -> p t h d", d=HD), ACT.Copy)
                nc.scalar.activation(v_sb[:, bass.ds(g * NS, NS)].rearrange("p t h d -> p t (h d)"),
                                     PS[:, 1:5, 256:384], ACT.Copy).then_inc(v_kept, 1)
                act.drain()

            def spread_high(slot, qk):
                part = qk_parts[slot][qk]
                nc.scalar.activation(part[:, :, (Q_HIGH, K_HIGH)[qk], :],
                                     part[:, :, HIGH:HIGH + 1, :].broadcast_to([P, NS * HEADS, 2, HD]), ACT.Copy).then_inc(high_spread, 1)

            def keep_turned_heads(gi, g, batches):
                for i in batches:
                    if i == 0:
                        act.wait_ge(q_stored, gi * 16 + ONE)
                    act.wait_ge(qk_turned, gi * 8 + (i + 1) + ONE)
                    keep_turned(nc.scalar.copy, g, i).then_inc(qk_kept_act, 1)

            def project(L):
                def group(g, slot, normed):
                    gi, gx = L * NB + g, L * 2 * NB + g
                    keep_turned_heads(gi, g, (0,))
                    keep_projected(gi + 1, g + 1, 1 - slot)
                    keep_turned_heads(gi, g, (2,))
                    spread_high(1 - slot, 0)
                    keep_turned_heads(gi, g, (4,))
                    spread_high(1 - slot, 1)
                    keep_turned_heads(gi, g, (6,))
                    if normed:
                        keep_normed(gx + 2, C_G1, C_BE1)

                keep_normed(L * 2 * NB, C_G1, C_BE1)
                keep_projected(L * NB, 0, None)
                spread_high(0, 0)
                spread_high(0, 1)
                keep_normed(L * 2 * NB + 1, C_G1, C_BE1)
                with act.Fori(0, (NB - 2) // 2) as pair:
                    for slot in range(2):
                        group(pair * 2 + slot, slot, True)
                group(NB - 2, 0, False)
                keep_turned_heads(L * NB + (NB - 1), NB - 1, (0, 2, 4, 6))

            def exp_pair(ib, pair):
                t, j = pair // 2, 2 * (pair % 2)
                slot = 2 * slot_of[("b", pair)]
                act.wait_ge(b_scored, ib * B_PAIRS + (pair + 1))
                if j == 0:
                    act.wait_ge(pv_done, ib * B_QUADS + (t - P_SLOTS + 1 + CREDIT_PV))
                nc.scalar.activation(p_buf[:, t % P_SLOTS, j:j + 2, :], ps_b[:, slot:slot + 2, :],
                                     ACT.Exp, scale=SCALE).then_inc(b_exped, 1)

            def keep_mask(ia, nb, q, c):
                act.wait_ge(mask_turned, ia * NC + (c + 1 + CREDIT_MASK))
                n = CHUNK // P
                nc.scalar.activation(mask_t[:, bass.ds((nb % 2) * MT + c * n, n), bass.ds(q * P, P)],
                                     ps_b[:, 2 * slot_of[("m", c)], :].bitcast(BF16).rearrange("p (m c) -> p m c", m=n),
                                     ACT.Copy).then_inc(mask_kept, 1)

            def make_mask01(ib, nb, q, s):
                act.wait_ge(p_masked, ib * B_POOLED + (len(POOL_OPS) * max(s - 1, 0) + ONE))
                nc.scalar.activation(mask01[:, s % 2, :],
                                     mask_t[:, bass.ds((nb % 2) * MT + q * STEPS + s, 1), :].rearrange("p a c -> p (a c)"),
                                     ACT.Copy, bias=1.0, scale=-1.0 / MASKED).then_inc(mask01_made, 1)

            def set_v(ib, q, s):
                act.wait_ge(pv_done, ib * B_QUADS + (2 * s - 2 + CREDIT_PV))
                nc.scalar.activation(v_cur[:, s % 2, :, 0:HD],
                                     v_sb[:, bass.ds(q * STEPS + s, 1), :, :].rearrange("p a h d -> p (a h) d"),
                                     ACT.Copy).then_inc(v_set, 1)

            def body(ia, ib, nba, nb, q, a, b):
                if b:
                    make_mask01(ib, nb, q, 0)
                for s in range(STEPS):
                    for k in range(4):
                        if a and s % 2 == 1 and k == 2:
                            keep_mask(ia, nba, q, s // 2)
                        if b:
                            exp_pair(ib, 4 * s + k)
                            if k == 0 and s + 1 < B_MASKS:
                                make_mask01(ib, nb, q, s + 1)
                            if k == 1:
                                set_v(ib, q, s)

            def keep_negs(ja, nb):
                act.wait_ge(neg_turned, ja + 1 + ONE)
                keep_neg(nc.scalar.copy, nb, 0).then_inc(neg_kept_act, 1)

            def store_o(jb, nb):
                act.wait_ge(pv_done, jb * (NS * B_QUADS) + (NS * B_QUADS + CREDIT_PV))
                act.wait_ge(o_stored, jb * 16 + ONE)
                nc.scalar.copy(o_sb[:, 0, :], ps_o[:, 0, :]).then_inc(o_kept_act, 1)
                act.wait_ge(o_kept_act, jb + 1 + ONE)
                act.wait_ge(o_kept_dve, jb + 1 + ONE)
                act.dma_start(o_dram[bass.ds(nb, 1)].rearrange("a p b c -> (a p) (b c)"),
                              o_sb[:].rearrange("p b c -> p (b c)")).then_inc(o_stored, 16)

            def attend(L):
                with act.Fori(0, NS) as q:
                    body(L * NB * NS + q, None, 0, None, q, True, False)
                keep_negs(L * NB, 0)
                with act.Fori(0, NB - 1) as nb:
                    with act.Fori(0, NS) as q:
                        ib = (L * NB + nb) * NS + q
                        body(ib + NS, ib, nb + 1, nb, q, True, True)
                    store_o(L * NB + nb, nb)
                    keep_negs(L * NB + nb + 1, nb + 1)
                with act.Fori(0, NS) as q:
                    body(None, (L * NB + (NB - 1)) * NS + q, None, NB - 1, q, False, True)
                store_o(L * NB + (NB - 1), NB - 1)
                act.wait_ge(o_stored, (L + 1) * NB * 16 + ONE)
                act.sem_inc(seen, 1)

            def keep_attn(gi):
                act.wait_ge(attn_turned, gi + 1 + ONE)
                act.wait_ge(proj_ready, gi + ONE)
                nc.scalar.copy(attn_t, PS[:, 1, :]).then_inc(attn_kept, 1)

            def gelu(gi, f):
                if f == 0:
                    act.wait_ge(ff_ready, gi + ONE)
                act.wait_ge(hid_ready, gi * 4 + (f + 1) + ONE)
                nc.scalar.activation(g_t[:, f, :], PS[:, 4 + f, :], ACT.Gelu_apprx_tanh,
                                     bias=wts[:, C_B1 + f:C_B1 + f + 1]).then_inc(gelu_done, 1)

            def feed_forward(L):
                keep_attn(L * NB)
                with act.Fori(0, NB - 1) as g:
                    gi, gx = L * NB + g, (L * 2 + 1) * NB + g
                    act.wait_ge(hid_ready, gi * 4 + ONE)
                    keep_normed(gx, C_G2, C_BE2)
                    for f in range(3):
                        gelu(gi, f)
                    keep_attn(gi + 1)
                    gelu(gi, 3)
                gi, gx = L * NB + (NB - 1), (L * 2 + 1) * NB + (NB - 1)
                act.wait_ge(hid_ready, gi * 4 + ONE)
                keep_normed(gx, C_G2, C_BE2)
                for f in range(4):
                    gelu(gi, f)

            with act.Fori(0, LAYERS) as L:
                act.wait_ge(w_here, L * 32 + 16)
                project(L)
                phase_barrier(act, L, 0)
                attend(L)
                phase_barrier(act, L, 1)
                act.wait_ge(w_here, L * 32 + 32)
                feed_forward(L)
                phase_barrier(act, L, 2)

        @block.vector
        def _(dve):
            for s in from_one["dve"]:
                dve.sem_inc(s, ONE)
            dve.sem_inc(a_maxed, CREDIT_MAXED)
            dve.sem_inc(mask_made, CREDIT_MASK)

            def until(s, value):
                dve.wait_ge(s, value)
                dve.sem_inc(seen, 1)

            dve.memset(zeros[:], 0.0)
            dve.memset(minus_half[:], -0.5)
            dve.memset(v_cur[:], 0.0)
            dve.memset(rlast[:], 0.0)
            dve.drain()
            dve.memset(v_cur[:, :, :, HD:HD + 1], 1.0)
            dve.drain().then_inc(set_up, 4)

            def norm_stats(src, gx):
                for t in range(NS):
                    dve.bn_stats(stats[:, t, :], src[:, t, :])
                dve.drain()
                for t in range(NS):
                    last = dve.bn_aggr(mv[:, t, :], stats[:, t, :])
                last.then_inc(var_ready, 1)

            def norm_rows(src, gx):
                until(rstd_ready, gx + 1)
                until(xn_turned, gx + ONE)
                for t in range(NS):
                    last = dve.tensor_scalar(xn[:, t, :], src[:, t, :], mv[:, t, 0:1], rstd[:, t:t + 1],
                                             ALU.subtract, ALU.mult)
                last.then_inc(xn_ready, 1)

            def take_high(gi, slot):
                until(v_kept, gi + 1 + ONE)
                for part, left, first in zip(qk_parts[slot], (q_rest, k_rest), (0, P)):
                    dve.tensor_tensor(left.rearrange("p (t h) d -> p t h d", t=NS),
                                      PS[:, 1:5, first:first + P].rearrange("p t (h d) -> p t h d", d=HD),
                                      part[:, :, HIGH, :].rearrange("p (t h) d -> p t h d", t=NS), ALU.subtract)
                dve.drain().then_inc(qk_taken, 1)

            def make_middle(slot):
                dve.tensor_copy(parts[slot][:, :, MIDDLE, :], rest)
                dve.drain()

            def make_low(slot, qk):
                part, left = qk_parts[slot][qk], (q_rest, k_rest)[qk]
                dve.tensor_tensor(part[:, :, (Q_LOW, K_LOW)[qk], :], left, part[:, :, MIDDLE, :], ALU.subtract)
                dve.tensor_copy(part[:, :, (Q_MIDDLE, K_MIDDLE)[qk], :], part[:, :, MIDDLE, :])
                if qk == 1:
                    dve.drain().then_inc(parts_ready, 1)

            def keep_turned_heads(gi, g, batches):
                for i in batches:
                    if i == 1:
                        until(q_stored, gi * 16 + ONE)
                    until(qk_turned, gi * 8 + (i + 1) + ONE)
                    keep_turned(dve.tensor_copy, g, i).then_inc(qk_kept_dve, 1)

            def project(L):
                def group(g, slot, normed):
                    gi, gx = L * NB + g, L * 2 * NB + g
                    keep_turned_heads(gi, g, (1,))
                    if normed:
                        until(x_loaded, (gx + 2) * 16 + 16)
                        norm_stats(xt, gx + 2)
                    keep_turned_heads(gi, g, (3,))
                    if normed:
                        norm_rows(xt, gx + 2)
                    take_high(gi + 1, 1 - slot)
                    keep_turned_heads(gi, g, (5,))
                    make_middle(1 - slot)
                    make_low(1 - slot, 0)
                    keep_turned_heads(gi, g, (7,))
                    make_low(1 - slot, 1)

                for i in range(2):
                    gx = L * 2 * NB + i
                    until(x_loaded, gx * 16 + 16)
                    norm_stats(xt, gx)
                    norm_rows(xt, gx)
                take_high(L * NB, 0)
                make_middle(0)
                make_low(0, 0)
                make_low(0, 1)
                with dve.Fori(0, (NB - 2) // 2) as pair:
                    for slot in range(2):
                        group(pair * 2 + slot, slot, True)
                group(NB - 2, 0, False)
                keep_turned_heads(L * NB + (NB - 1), NB - 1, (1, 3, 5, 7))

            def make_mask(ia, c, first=False):
                until(adj_loaded[c % 2], ia * (NC // 2 * 16) + (c // 2 + 1) * 16)
                until(mask_turned, ia * NC + (c - 1 + CREDIT_MASK))
                if not first:
                    until(a_maxed, ia * A_BLOCKS + (2 * HEADS * (c - 1) + CREDIT_MAXED))
                dve.tensor_scalar(mask_n[:, c % 2, :], adj_in[:, c % 2, :], 0.0, MASKED,
                                  ALU.is_equal, ALU.mult).then_inc(mask_made, 1)

            def keep_max(ia, q):
                until(a_maxed, ia * A_BLOCKS + CREDIT_MAXED)
                dve.tensor_scalar(neg[:, bass.ds(q * HEADS, HEADS)], rlast[:], -1.0, None, ALU.mult).then_inc(neg_set, 1)

            def body(ia, q, jn, alone):
                for mb in range(MB):
                    c = mb // 2
                    if mb % 2 == 0:
                        until(mask_made, ia * NC + (c + 1 + CREDIT_MASK))
                    for h in range(HEADS):
                        k = mb * HEADS + h
                        if mb == 0 and h == 4:
                            keep_max(ia, q)
                        if mb % 2 == 1 and h == 4:
                            make_mask(ia + (c + 1) // NC, (c + 1) % NC)
                        if mb == MB - 1 and h == 0:
                            until(neg_set, jn + (1 + ONE))
                        until(a_maxed, ia * A_BLOCKS + (k + 1 - SPILLS + CREDIT_MAXED))
                        until(a_scored, ia * A_BLOCKS + (k + 1 + CREDIT_SCORED))
                        first = LOWEST if mb == 0 else rmax[:, h:h + 1]
                        into = rlast if mb == MB - 1 else rmax
                        dve.tensor_tensor_reduce(spill[:, k % SPILLS, :], a_bank(k, alone)[0],
                                                 mask_n[:, c % 2, (mb % 2) * TILE:(mb % 2 + 1) * TILE],
                                                 1.0, first, ALU.add, ALU.max, into[:, h:h + 1]).then_inc(a_maxed, 1)

            def sub_blocks(ja, nb, alone):
                with dve.Fori(0, NS) as q:
                    body(ja * NS + q, q, ja * (NS + 1) + q, alone)
                keep_max((ja + 1) * NS, NS)
                until(neg_set, ja * (NS + 1) + (NS + 1 + ONE))
                split_neg(ja, nb)

            def split_neg(ja, nb):
                n3 = neg[:, HEADS:].rearrange("p (t h) -> p t h", t=NS)
                until(neg_turned, ja + ONE)
                dve.tensor_copy(neg_p[:, :, 0, :], n3)
                dve.drain()
                dve.tensor_tensor(n3, n3, neg_p[:, :, 0, :], ALU.subtract)
                dve.drain()
                dve.tensor_copy(neg_p[:, :, 1, :], n3)
                dve.drain()
                dve.tensor_tensor(neg_p[:, :, 2, :], n3, neg_p[:, :, 1, :], ALU.subtract).then_inc(neg_ready, 1)

            def keep_negs(ja, nb):
                until(neg_turned, ja + 1 + ONE)
                for i in (1, 2, 3):
                    keep_neg(dve.tensor_copy, nb, i).then_inc(neg_kept_dve, 1)

            def keep_o(jb):
                until(pv_done, jb * (NS * B_QUADS) + (NS * B_QUADS + CREDIT_PV))
                until(o_stored, jb * 16 + ONE)
                dve.tensor_copy(o_sb[:, 1, :], ps_o[:, 1, :]).then_inc(o_kept_dve, 1)

            def attend(L):
                sub_blocks(L * NB, 0, True)
                keep_negs(L * NB, 0)
                with dve.Fori(0, NB - 1) as nb:
                    sub_blocks(L * NB + nb + 1, nb + 1, False)
                    keep_o(L * NB + nb)
                    keep_negs(L * NB + nb + 1, nb + 1)
                keep_o(L * NB + (NB - 1))

            x2v = x2.rearrange("p (t c) -> p t c", t=NS)

            def row_bias(col):
                return wts[:, col:col + P].rearrange("p (a c) -> p a c", a=1).broadcast_to([P, NS, P])

            def normalise(gi):
                until(o_turned, gi + 1 + ONE)
                rows = PS[:, 1:3, :].rearrange("p b (g d) -> p (b g) d", d=32)
                sums = rsum.rearrange("p (g d) -> p g d", d=1)
                dve.reciprocal(sums, rows[:, :, HD:HD + 1])
                dve.drain()
                until(attn_turned, gi + ONE)
                dve.tensor_tensor(attn.rearrange("p (g d) -> p g d", d=HD), rows[:, :, 0:HD],
                                  sums.broadcast_to([P, NS * HEADS, HD]), ALU.mult).then_inc(attn_ready, 1)

            def first_half(gi, gx):
                normalise(gi)
                until(x_loaded, gx * 16 + 16)
                dve.tensor_tensor(x2v, xt, row_bias(C_BP), ALU.add)
                dve.drain()
                until(proj_ready, gi + 1 + ONE)
                dve.tensor_tensor(x2, PS[:, 2, :], x2, ALU.add)
                dve.drain()
                norm_stats(x2v, gx)
                norm_rows(x2v, gx)

            def add_output_bias():
                dve.tensor_tensor(x2_b.rearrange("p (t c) -> p t c", t=NS), x2v, row_bias(C_B2), ALU.add)
                dve.drain()

            def second_half(gi):
                until(ff_ready, gi + 1 + ONE)
                until(out_stored, gi * 16 + ONE)
                dve.tensor_tensor(x3, PS[:, 3, :], x2_b, ALU.add).then_inc(x3_ready, 1)
                dve.drain()

            def feed_forward(L):
                first_half(L * NB, (L * 2 + 1) * NB)
                add_output_bias()
                with dve.Fori(0, NB - 1) as g:
                    first_half(L * NB + g + 1, (L * 2 + 1) * NB + g + 1)
                    second_half(L * NB + g)
                    add_output_bias()
                second_half(L * NB + (NB - 1))

            make_mask(0, 0, first=True)
            with dve.Fori(0, LAYERS) as L:
                until(w_here, L * 32 + 16)
                project(L)
                phase_barrier(dve, L, 0)
                attend(L)
                phase_barrier(dve, L, 1)
                until(w_here, L * 32 + 32)
                feed_forward(L)
                phase_barrier(dve, L, 2)

        @block.gpsimd
        def _(pool):
            for s in from_one["pool"]:
                pool.sem_inc(s, ONE)
            pool.wait_ge(set_up, 5)

            def rstds(gx0):
                with pool.Fori(0, NB) as g:
                    pool.wait_ge(var_ready, gx0 + g + 1)
                    pool.sem_inc(seen, 1)
                    pool.tensor_scalar(ve, mv[:, :, 1], EPS, None, ALU.add)
                    pool.drain()
                    pool.tensor_tensor(rstd, ve, minus_half[:], ALU.pow).then_inc(rstd_ready, 1)

            def masks(L):
                def sub_block(ib, ops):
                    for s in range(B_MASKS):
                        for i, (h, n) in enumerate(ops):
                            t, j = 2 * s + h // 4, h % 4
                            if i == 0:
                                pool.wait_ge(mask01_made, ib * B_MASKS + (s + 1))
                                pool.sem_inc(seen, 1)
                            pool.wait_ge(b_exped, ib * B_PAIRS + (4 * s + h // 2 + 1 + CREDIT_EXPED))
                            p = p_buf[:, t % P_SLOTS, j:j + n, :].bitcast(I32)
                            pool.tensor_tensor(p, p, mask01[:, s % 2, :].rearrange("p (a c) -> p a c", a=1).broadcast_to([P, n, TILE]),
                                               ALU.mult).then_inc(p_masked, 1)

                with pool.Fori(0, (NB - 1) * NS) as i:
                    sub_block(L * NB * NS + i, POOL_OPS)
                with pool.Fori((NB - 1) * NS, NB * NS) as i:
                    sub_block(L * NB * NS + i, POOL_OPS_LAST)

            with pool.Fori(0, LAYERS) as L:
                rstds(L * 2 * NB)
                phase_barrier(pool, L, 0)
                masks(L)
                phase_barrier(pool, L, 1)
                rstds((L * 2 + 1) * NB)
                phase_barrier(pool, L, 2)


def kernel(**inputs):
    import numpy as np
    import ml_dtypes
    import concourse.bacc as bacc
    from concourse.bass_utils import run_bass_kernel_spmd

    nc = bacc.Bacc("TRN2", target_bir_lowering=False, num_devices=1, dynamic_dma_scratch_size=1024)
    arrays, aps = {}, {}

    def give(name, a):
        a = np.ascontiguousarray(a)
        arrays[f"in_{name}"] = a
        aps[name] = nc.dram_tensor(f"in_{name}", a.shape, mybir.dt.from_np(a.dtype), kind="ExternalInput").ap()
        return aps[name]

    give("x", inputs["x"])
    give("adj", inputs["adj"])
    weights = [{n: give(f"L{l}_gnn_{n}", inputs[f"L{l}_gnn_{n}"]) for n in NAMES} for l in range(LAYERS)]
    ident = give("ident", np.eye(P, dtype=ml_dtypes.bfloat16))
    ident_f = give("ident_f", np.eye(P, dtype=np.float32))
    rows = np.zeros((P - KROWS, HEADS, TILE), ml_dtypes.bfloat16)
    for i in range(MROWS):
        rows[i, i % HEADS] = 1.0
    head_rows = give("head_rows", rows)
    out = nc.dram_tensor("out_dram", (N, P), F32, kind="ExternalOutput").ap()
    gnn_kernel(nc, aps["x"], aps["adj"], weights, ident, ident_f, head_rows, out)
    r = run_bass_kernel_spmd(nc, [arrays], core_ids=[0])
    return r.results[0]["out_dram"]
```
